# Optimizing a Trainium2 kernel written in Bass

```python
import numpy as np
import jax
import jax.numpy as jnp

def _softmax(x, axis=-1):
    return jax.nn.softmax(x, axis=axis)

def _gelu(x):
    return jax.nn.gelu(x, approximate=True)

def _silu(x):
    return jax.nn.silu(x)

def _sigmoid(x):
    return jax.nn.sigmoid(x)

def _layernorm(x, axis=-1, eps=1e-05):
    m = jnp.mean(x, axis=axis, keepdims=True)
    v = jnp.var(x, axis=axis, keepdims=True)
    return (x - m) / jnp.sqrt(v + eps)

def _scatter_add(tgt, idx, src, axis=0):
    return tgt.at[idx].add(src)

def _segment_sum(src, seg, n):
    return jax.ops.segment_sum(src, seg, n)
kernel_name = 'mk_seq_preln_d4_jaxref_r8_6b16f7'

def setup_inputs(seed: int=0):
    np.random.seed(seed)
    _w = jnp.asarray

    def _L0_attn_setup():
        import jax, jax.numpy as jnp
        import numpy as np
        D_MODEL, N_QUERY, N_HEAD = (128, 2, 8)
        D_HEAD = D_MODEL // (N_QUERY * N_HEAD)
        KV = D_HEAD * N_HEAD

        def _reference_tuple_inner(x, Wq, Wk, Wv, memory, memory_norm, memory_weight):
            B, S, _ = x.shape
            QH = N_QUERY * N_HEAD
            scale = 1.0 / jnp.sqrt(jnp.float32(D_HEAD))
            q = x @ Wq
            k = x @ Wk
            v = x @ Wv
            q4 = q.reshape(B, S, QH, D_HEAD)
            k4 = jnp.repeat(k.reshape(B, S, N_HEAD, D_HEAD), N_QUERY, axis=2)
            v4 = jnp.repeat(v.reshape(B, S, N_HEAD, D_HEAD), N_QUERY, axis=2)
            scores = jnp.einsum('bsnd,btnd->bnst', q4, k4) * scale
            probs = jax.nn.softmax(scores, axis=-1)
            a_dot = jnp.einsum('bnst,btnd->bsnd', probs, v4)
            sigma_q = jax.nn.elu(q.reshape(B, S, N_QUERY, KV))
            num = sigma_q @ memory
            den = (sigma_q @ memory_norm)[..., None]
            a_mem = (num / den).reshape(B, S, QH, D_HEAD)
            sigma_k = jax.nn.elu(k)
            retrieved = sigma_k @ memory / (sigma_k @ memory_norm)[..., None]
            new_memory = memory + jnp.einsum('bsk,bsv->kv', sigma_k, v - retrieved)
            new_memory_norm = memory_norm + jnp.sum(sigma_k, axis=(0, 1))
            w = jax.nn.sigmoid(memory_weight)
            out = (a_dot * (1.0 - w) + a_mem * w).reshape(B, S, D_MODEL)
            return (out, new_memory, new_memory_norm)
        key = jax.random.key(seed)
        ks = jax.random.split(key, 6)
        B, S = (2, 256)
        x = jax.random.normal(ks[0], (B, S, D_MODEL), jnp.float32)
        Wq = jax.random.normal(ks[1], (D_MODEL, D_MODEL), jnp.float32) / np.sqrt(D_MODEL)
        Wk = jax.random.normal(ks[2], (D_MODEL, KV), jnp.float32) / np.sqrt(D_MODEL)
        Wv = jax.random.normal(ks[3], (D_MODEL, KV), jnp.float32) / np.sqrt(D_MODEL)
        memory = jax.random.normal(ks[4], (KV, KV), jnp.float32)
        memory_norm = jnp.ones((KV,), jnp.float32)
        memory_weight = jnp.ones((1,), jnp.float32)
        return {'x': x, 'Wq': Wq, 'Wk': Wk, 'Wv': Wv, 'memory': memory, 'memory_norm': memory_norm, 'memory_weight': memory_weight}
    _L0_attn_in = _L0_attn_setup()

    def _L0_ffn_setup():
        import jax, jax.numpy as jnp
        import numpy as np
        B, S, D, H, E = (4, 256, 128, 512, 8)
        EPS = 1e-12

        def _wn(v, g):
            n = jnp.sqrt(jnp.sum(v * v, axis=-1, keepdims=True))
            return v / jnp.maximum(n, EPS) * g[:, None]
        key = jax.random.key(seed)
        ks = jax.random.split(key, 8)
        return {'x': jax.random.normal(ks[0], (B, S, D), dtype=jnp.float32), 'gate_v': jax.random.normal(ks[1], (E, D), dtype=jnp.float32), 'gate_g': jnp.ones((E,), dtype=jnp.float32), 'gate_b': jnp.zeros((E,), dtype=jnp.float32), 'w1_v': jax.random.normal(ks[2], (E, H, D), dtype=jnp.float32), 'w1_g': jnp.ones((E, H), dtype=jnp.float32), 'b1': jnp.zeros((E, H), dtype=jnp.float32), 'w2_v': jax.random.normal(ks[3], (E, D, H), dtype=jnp.float32), 'w2_g': jnp.ones((E, D), dtype=jnp.float32), 'b2': jnp.zeros((E, D), dtype=jnp.float32)}
    _L0_ffn_in = _L0_ffn_setup()

    def _L1_attn_setup():
        import jax, jax.numpy as jnp
        import numpy as np
        EMB = 128
        HEADS = 16
        EPS = 1e-05

        def layer_norm(x):
            mu = jnp.mean(x, axis=-1, keepdims=True)
            var = jnp.var(x, axis=-1, keepdims=True)
            return (x - mu) / jnp.sqrt(var + EPS)

        def pattention(x, K, V):
            scale = EMB ** (-0.5)
            a = jax.nn.softmax(scale * jnp.einsum('btc,nc->btn', x, K), axis=-1)
            return jnp.einsum('btn,nc->btc', a, V)

        def causal_sdpa(q, k, v):
            T = q.shape[2]
            d = q.shape[-1]
            scores = jnp.einsum('bhqd,bhkd->bhqk', q, k) / jnp.sqrt(jnp.asarray(d, q.dtype))
            mask = jnp.tril(jnp.ones((T, T), dtype=bool))
            scores = jnp.where(mask, scores, jnp.asarray(-jnp.inf, q.dtype))
            attn = jax.nn.softmax(scores, axis=-1)
            return jnp.einsum('bhqk,bhkd->bhqd', attn, v)
        key = jax.random.key(seed)
        ks = jax.random.split(key, 11)
        B, T, C = (2, 256, EMB)
        N = 256 // 2
        inp = {'x': jax.random.normal(ks[0], (B, T, C), dtype=jnp.float32)}
        names = ['qK', 'qV', 'kK', 'kV', 'vK', 'vV', 'pK', 'pV']
        for i, nm in enumerate(names):
            inp[nm] = jax.random.normal(ks[1 + i], (N, C), dtype=jnp.float32)
        inp['fK'] = jax.random.normal(ks[9], (4 * N, C), dtype=jnp.float32)
        inp['fV'] = jax.random.normal(ks[10], (4 * N, C), dtype=jnp.float32)
        return inp
    _L1_attn_in = _L1_attn_setup()

    def _L1_ffn_setup():
        import jax, jax.numpy as jnp
        import numpy as np
        DIM = 128
        NUM_EXPERTS = 6
        TOP_K = 2
        HIDDEN = DIM * 2
        key = jax.random.key(seed)
        ks = jax.random.split(key, 7)
        s_in = 1.0 / np.sqrt(DIM)
        s_h = 1.0 / np.sqrt(HIDDEN)
        x = jax.random.normal(ks[0], (4, 256, DIM), dtype=jnp.float32)
        Wg = jax.random.uniform(ks[1], (DIM, NUM_EXPERTS), jnp.float32, -s_in, s_in)
        bg = jax.random.uniform(ks[2], (NUM_EXPERTS,), jnp.float32, -s_in, s_in)
        W1 = jax.random.uniform(ks[3], (NUM_EXPERTS, DIM, HIDDEN), jnp.float32, -s_in, s_in)
        b1 = jax.random.uniform(ks[4], (NUM_EXPERTS, HIDDEN), jnp.float32, -s_in, s_in)
        W2 = jax.random.uniform(ks[5], (NUM_EXPERTS, HIDDEN, DIM), jnp.float32, -s_h, s_h)
        b2 = jax.random.uniform(ks[6], (NUM_EXPERTS, DIM), jnp.float32, -s_h, s_h)
        return {'x': x, 'Wg': Wg, 'bg': bg, 'W1': W1, 'b1': b1, 'W2': W2, 'b2': b2}
    _L1_ffn_in = _L1_ffn_setup()

    def _L2_attn_setup():
        import jax, jax.numpy as jnp
        from jax import lax
        import numpy as np
        D_MODEL = 128
        D_STATE = 16
        D_CONV = 4
        EXPAND = 2
        D_INNER = EXPAND * D_MODEL
        DT_RANK = D_MODEL // 16
        B, L = (1, 128)

        def _mamba(x, in_w, conv_w, conv_b, xproj_w, dt_w, dt_b, Alog, Dp, out_w):
            xz = x @ in_w.T
            xi, z = jnp.split(xz, 2, axis=-1)
            xc = lax.conv_general_dilated(jnp.swapaxes(xi, 1, 2), conv_w, (1,), [(D_CONV - 1, 0)], feature_group_count=D_INNER)
            u = jnp.swapaxes(jax.nn.silu(xc + conv_b[None, :, None]), 1, 2)
            x_dbl = u @ xproj_w.T
            dt = x_dbl[..., :DT_RANK]
            Bm = x_dbl[..., DT_RANK:DT_RANK + D_STATE]
            Cm = x_dbl[..., DT_RANK + D_STATE:]
            delta = jax.nn.softplus(dt @ dt_w.T + dt_b)
            A = -jnp.exp(Alog)
            dA = jnp.exp(jnp.einsum('bld,dn->bldn', delta, A))
            dBu = jnp.einsum('bld,bln,bld->bldn', delta, Bm, u)

            def step(h, inputs):
                a, b, c = inputs
                h = a * h + b
                return (h, jnp.einsum('bdn,bn->bd', h, c))
            h0 = jnp.zeros((x.shape[0], D_INNER, D_STATE), x.dtype)
            _, ys = lax.scan(step, h0, (jnp.moveaxis(dA, 1, 0), jnp.moveaxis(dBu, 1, 0), jnp.moveaxis(Cm, 1, 0)))
            y = jnp.moveaxis(ys, 0, 1) + u * Dp
            return y * jax.nn.silu(z) @ out_w.T

        def _block(x, fw_in_w, fw_conv_w, fw_conv_b, fw_xproj_w, fw_dt_w, fw_dt_b, fw_Alog, fw_Dp, fw_out_w, bw_in_w, bw_conv_w, bw_conv_b, bw_xproj_w, bw_dt_w, bw_dt_b, bw_Alog, bw_Dp, bw_out_w, proj_w, proj_b, ln_w, ln_b):
            out_fw = _mamba(x, fw_in_w, fw_conv_w, fw_conv_b, fw_xproj_w, fw_dt_w, fw_dt_b, fw_Alog, fw_Dp, fw_out_w) + x
            xb = jnp.flip(x, axis=1)
            out_bw = jnp.flip(_mamba(xb, bw_in_w, bw_conv_w, bw_conv_b, bw_xproj_w, bw_dt_w, bw_dt_b, bw_Alog, bw_Dp, bw_out_w) + xb, axis=1)
            out = jnp.concatenate([out_fw, out_bw], axis=-1) @ proj_w.T + proj_b
            mu = out.mean(-1, keepdims=True)
            var = out.var(-1, keepdims=True)
            return (out - mu) / jnp.sqrt(var + 1e-05) * ln_w + ln_b
        key = jax.random.key(seed)
        ks = jax.random.split(key, 8)

        def nrm(k, shape, s=0.02):
            return jax.random.normal(k, shape, jnp.float32) * s

        def mamba_params(kbase):
            k = jax.random.split(kbase, 7)
            return {'in_w': nrm(k[0], (2 * D_INNER, D_MODEL)), 'conv_w': nrm(k[1], (D_INNER, 1, D_CONV), 0.1), 'conv_b': nrm(k[2], (D_INNER,), 0.1), 'xproj_w': nrm(k[3], (DT_RANK + 2 * D_STATE, D_INNER)), 'dt_w': nrm(k[4], (D_INNER, DT_RANK), 0.1), 'dt_b': nrm(k[5], (D_INNER,), 0.1), 'Alog': jnp.log(jnp.broadcast_to(jnp.arange(1.0, D_STATE + 1, dtype=jnp.float32), (D_INNER, D_STATE))), 'Dp': jnp.ones((D_INNER,), jnp.float32), 'out_w': nrm(k[6], (D_MODEL, D_INNER))}
        fw = mamba_params(ks[0])
        bw = mamba_params(ks[1])
        inp = {'x': jax.random.normal(ks[2], (B, L, D_MODEL), jnp.float32)}
        for n, p in fw.items():
            inp['fw_' + n] = p
        for n, p in bw.items():
            inp['bw_' + n] = p
        inp['proj_w'] = nrm(ks[3], (D_MODEL, 2 * D_MODEL))
        inp['proj_b'] = jnp.zeros((D_MODEL,), jnp.float32)
        inp['ln_w'] = jnp.ones((D_MODEL,), jnp.float32)
        inp['ln_b'] = jnp.zeros((D_MODEL,), jnp.float32)
        return inp
    _L2_attn_in = _L2_attn_setup()

    def _L2_ffn_setup():
        import jax, jax.numpy as jnp
        import numpy as np
        B, S, D, E, H, K = (4, 256, 128, 8, 64, 2)
        key = jax.random.key(seed)
        ks = jax.random.split(key, 11)
        sc = 0.02
        return {'x': jax.random.normal(ks[0], (B, S, D), dtype=jnp.float32), 'gate_W': jax.random.normal(ks[1], (D, E), dtype=jnp.float32) * sc, 'W1': jax.random.normal(ks[2], (E, D, H), dtype=jnp.float32) * sc, 'b1': jnp.zeros((E, H), dtype=jnp.float32), 'W2': jax.random.normal(ks[3], (E, H, D), dtype=jnp.float32) * sc, 'b2': jnp.zeros((E, D), dtype=jnp.float32), 'Ws1': jax.random.normal(ks[4], (D, H), dtype=jnp.float32) * sc, 'bs1': jnp.zeros((H,), dtype=jnp.float32), 'Ws2': jax.random.normal(ks[5], (H, D), dtype=jnp.float32) * sc, 'bs2': jnp.zeros((D,), dtype=jnp.float32), 'route_scale': jnp.ones((), dtype=jnp.float32)}
    _L2_ffn_in = _L2_ffn_setup()

    def _L3_attn_setup():
        import jax, jax.numpy as jnp
        import numpy as np
        B, S, H, D = (4, 256, 128, 128)
        key = jax.random.key(seed)
        k0, k1, k2, k3 = jax.random.split(key, 4)
        x = jax.random.normal(k0, (B, S, H), dtype=jnp.float32)
        scale = 1.0 / np.sqrt(H)
        Wq = jax.random.normal(k1, (D, H), dtype=jnp.float32) * scale
        Wk = jax.random.normal(k2, (D, H), dtype=jnp.float32) * scale
        Wv = jax.random.normal(k3, (D, H), dtype=jnp.float32) * scale
        return {'x': x, 'Wq': Wq, 'Wk': Wk, 'Wv': Wv}
    _L3_attn_in = _L3_attn_setup()

    def _L3_ffn_setup():
        import jax, jax.numpy as jnp
        import numpy as np
        B, S, D = (2, 64, 128)
        E, K, I = (16, 8, 128)
        I_SH = 128
        ROUTE_SCALE = 2.826
        key = jax.random.key(seed)
        ks = jax.random.split(key, 8)
        s = 0.02
        return {'x': jax.random.normal(ks[0], (B, S, D), dtype=jnp.float32), 'gate_w': jax.random.normal(ks[1], (E, D), dtype=jnp.float32) * s, 'expert_bias': jnp.zeros((E,), dtype=jnp.float32), 'w_gate': jax.random.normal(ks[2], (E, I, D), dtype=jnp.float32) * s, 'w_up': jax.random.normal(ks[3], (E, I, D), dtype=jnp.float32) * s, 'w_down': jax.random.normal(ks[4], (E, D, I), dtype=jnp.float32) * s, 'shared_gate_w': jax.random.normal(ks[5], (I_SH, D), dtype=jnp.float32) * s, 'shared_up_w': jax.random.normal(ks[6], (I_SH, D), dtype=jnp.float32) * s, 'shared_down_w': jax.random.normal(ks[7], (D, I_SH), dtype=jnp.float32) * s}
    _L3_ffn_in = _L3_ffn_setup()
    _d = {'L0_attn_x': _L0_attn_in['x'], 'L0_attn_Wq': _L0_attn_in['Wq'], 'L0_attn_Wk': _L0_attn_in['Wk'], 'L0_attn_Wv': _L0_attn_in['Wv'], 'L0_attn_memory': _L0_attn_in['memory'], 'L0_attn_memory_norm': _L0_attn_in['memory_norm'], 'L0_attn_memory_weight': _L0_attn_in['memory_weight'], 'L0_ffn_gate_v': _L0_ffn_in['gate_v'], 'L0_ffn_gate_g': _L0_ffn_in['gate_g'], 'L0_ffn_gate_b': _L0_ffn_in['gate_b'], 'L0_ffn_w1_v': _L0_ffn_in['w1_v'], 'L0_ffn_w1_g': _L0_ffn_in['w1_g'], 'L0_ffn_b1': _L0_ffn_in['b1'], 'L0_ffn_w2_v': _L0_ffn_in['w2_v'], 'L0_ffn_w2_g': _L0_ffn_in['w2_g'], 'L0_ffn_b2': _L0_ffn_in['b2'], 'L1_attn_qK': _L1_attn_in['qK'], 'L1_attn_qV': _L1_attn_in['qV'], 'L1_attn_kK': _L1_attn_in['kK'], 'L1_attn_kV': _L1_attn_in['kV'], 'L1_attn_vK': _L1_attn_in['vK'], 'L1_attn_vV': _L1_attn_in['vV'], 'L1_attn_pK': _L1_attn_in['pK'], 'L1_attn_pV': _L1_attn_in['pV'], 'L1_attn_fK': _L1_attn_in['fK'], 'L1_attn_fV': _L1_attn_in['fV'], 'L1_ffn_Wg': _L1_ffn_in['Wg'], 'L1_ffn_bg': _L1_ffn_in['bg'], 'L1_ffn_W1': _L1_ffn_in['W1'], 'L1_ffn_b1': _L1_ffn_in['b1'], 'L1_ffn_W2': _L1_ffn_in['W2'], 'L1_ffn_b2': _L1_ffn_in['b2'], 'L2_attn_fw_in_w': _L2_attn_in['fw_in_w'], 'L2_attn_fw_conv_w': _L2_attn_in['fw_conv_w'], 'L2_attn_fw_conv_b': _L2_attn_in['fw_conv_b'], 'L2_attn_fw_xproj_w': _L2_attn_in['fw_xproj_w'], 'L2_attn_fw_dt_w': _L2_attn_in['fw_dt_w'], 'L2_attn_fw_dt_b': _L2_attn_in['fw_dt_b'], 'L2_attn_fw_Alog': _L2_attn_in['fw_Alog'], 'L2_attn_fw_Dp': _L2_attn_in['fw_Dp'], 'L2_attn_fw_out_w': _L2_attn_in['fw_out_w'], 'L2_attn_bw_in_w': _L2_attn_in['bw_in_w'], 'L2_attn_bw_conv_w': _L2_attn_in['bw_conv_w'], 'L2_attn_bw_conv_b': _L2_attn_in['bw_conv_b'], 'L2_attn_bw_xproj_w': _L2_attn_in['bw_xproj_w'], 'L2_attn_bw_dt_w': _L2_attn_in['bw_dt_w'], 'L2_attn_bw_dt_b': _L2_attn_in['bw_dt_b'], 'L2_attn_bw_Alog': _L2_attn_in['bw_Alog'], 'L2_attn_bw_Dp': _L2_attn_in['bw_Dp'], 'L2_attn_bw_out_w': _L2_attn_in['bw_out_w'], 'L2_attn_proj_w': _L2_attn_in['proj_w'], 'L2_attn_proj_b': _L2_attn_in['proj_b'], 'L2_attn_ln_w': _L2_attn_in['ln_w'], 'L2_attn_ln_b': _L2_attn_in['ln_b'], 'L2_ffn_gate_W': _L2_ffn_in['gate_W'], 'L2_ffn_W1': _L2_ffn_in['W1'], 'L2_ffn_b1': _L2_ffn_in['b1'], 'L2_ffn_W2': _L2_ffn_in['W2'], 'L2_ffn_b2': _L2_ffn_in['b2'], 'L2_ffn_Ws1': _L2_ffn_in['Ws1'], 'L2_ffn_bs1': _L2_ffn_in['bs1'], 'L2_ffn_Ws2': _L2_ffn_in['Ws2'], 'L2_ffn_bs2': _L2_ffn_in['bs2'], 'L2_ffn_route_scale': _L2_ffn_in['route_scale'], 'L3_attn_Wq': _L3_attn_in['Wq'], 'L3_attn_Wk': _L3_attn_in['Wk'], 'L3_attn_Wv': _L3_attn_in['Wv'], 'L3_ffn_gate_w': _L3_ffn_in['gate_w'], 'L3_ffn_expert_bias': _L3_ffn_in['expert_bias'], 'L3_ffn_w_gate': _L3_ffn_in['w_gate'], 'L3_ffn_w_up': _L3_ffn_in['w_up'], 'L3_ffn_w_down': _L3_ffn_in['w_down'], 'L3_ffn_shared_gate_w': _L3_ffn_in['shared_gate_w'], 'L3_ffn_shared_up_w': _L3_ffn_in['shared_up_w'], 'L3_ffn_shared_down_w': _L3_ffn_in['shared_down_w']}
    _x0 = _d['L0_attn_x']
    _d['L0_attn_x'] = jax.random.normal(jax.random.fold_in(jax.random.key(seed), 1), (8, 512, 128), dtype=_x0.dtype)
    del _x0
    return _d

def reference(L0_attn_x, L0_attn_Wq, L0_attn_Wk, L0_attn_Wv, L0_attn_memory, L0_attn_memory_norm, L0_attn_memory_weight, L0_ffn_gate_v, L0_ffn_gate_g, L0_ffn_gate_b, L0_ffn_w1_v, L0_ffn_w1_g, L0_ffn_b1, L0_ffn_w2_v, L0_ffn_w2_g, L0_ffn_b2, L1_attn_qK, L1_attn_qV, L1_attn_kK, L1_attn_kV, L1_attn_vK, L1_attn_vV, L1_attn_pK, L1_attn_pV, L1_attn_fK, L1_attn_fV, L1_ffn_Wg, L1_ffn_bg, L1_ffn_W1, L1_ffn_b1, L1_ffn_W2, L1_ffn_b2, L2_attn_fw_in_w, L2_attn_fw_conv_w, L2_attn_fw_conv_b, L2_attn_fw_xproj_w, L2_attn_fw_dt_w, L2_attn_fw_dt_b, L2_attn_fw_Alog, L2_attn_fw_Dp, L2_attn_fw_out_w, L2_attn_bw_in_w, L2_attn_bw_conv_w, L2_attn_bw_conv_b, L2_attn_bw_xproj_w, L2_attn_bw_dt_w, L2_attn_bw_dt_b, L2_attn_bw_Alog, L2_attn_bw_Dp, L2_attn_bw_out_w, L2_attn_proj_w, L2_attn_proj_b, L2_attn_ln_w, L2_attn_ln_b, L2_ffn_gate_W, L2_ffn_W1, L2_ffn_b1, L2_ffn_W2, L2_ffn_b2, L2_ffn_Ws1, L2_ffn_bs1, L2_ffn_Ws2, L2_ffn_bs2, L2_ffn_route_scale, L3_attn_Wq, L3_attn_Wk, L3_attn_Wv, L3_ffn_gate_w, L3_ffn_expert_bias, L3_ffn_w_gate, L3_ffn_w_up, L3_ffn_w_down, L3_ffn_shared_gate_w, L3_ffn_shared_up_w, L3_ffn_shared_down_w):

    def _L0_attn_ref(x, Wq, Wk, Wv, memory, memory_norm, memory_weight):
        import jax, jax.numpy as jnp
        import numpy as np
        D_MODEL, N_QUERY, N_HEAD = (128, 2, 8)
        D_HEAD = D_MODEL // (N_QUERY * N_HEAD)
        KV = D_HEAD * N_HEAD

        def _reference_tuple_inner(x, Wq, Wk, Wv, memory, memory_norm, memory_weight):
            B, S, _ = x.shape
            QH = N_QUERY * N_HEAD
            scale = 1.0 / jnp.sqrt(jnp.float32(D_HEAD))
            q = x @ Wq
            k = x @ Wk
            v = x @ Wv
            q4 = q.reshape(B, S, QH, D_HEAD)
            k4 = jnp.repeat(k.reshape(B, S, N_HEAD, D_HEAD), N_QUERY, axis=2)
            v4 = jnp.repeat(v.reshape(B, S, N_HEAD, D_HEAD), N_QUERY, axis=2)
            scores = jnp.einsum('bsnd,btnd->bnst', q4, k4) * scale
            probs = jax.nn.softmax(scores, axis=-1)
            a_dot = jnp.einsum('bnst,btnd->bsnd', probs, v4)
            sigma_q = jax.nn.elu(q.reshape(B, S, N_QUERY, KV))
            num = sigma_q @ memory
            den = (sigma_q @ memory_norm)[..., None]
            a_mem = (num / den).reshape(B, S, QH, D_HEAD)
            sigma_k = jax.nn.elu(k)
            retrieved = sigma_k @ memory / (sigma_k @ memory_norm)[..., None]
            new_memory = memory + jnp.einsum('bsk,bsv->kv', sigma_k, v - retrieved)
            new_memory_norm = memory_norm + jnp.sum(sigma_k, axis=(0, 1))
            w = jax.nn.sigmoid(memory_weight)
            out = (a_dot * (1.0 - w) + a_mem * w).reshape(B, S, D_MODEL)
            return (out, new_memory, new_memory_norm)
        return _reference_tuple_inner(x, Wq, Wk, Wv, memory, memory_norm, memory_weight)[0]

    def _L0_ffn_ref(x, gate_v, gate_g, gate_b, w1_v, w1_g, b1, w2_v, w2_g, b2):
        import jax, jax.numpy as jnp
        import numpy as np
        B, S, D, H, E = (4, 256, 128, 512, 8)
        EPS = 1e-12

        def _wn(v, g):
            n = jnp.sqrt(jnp.sum(v * v, axis=-1, keepdims=True))
            return v / jnp.maximum(n, EPS) * g[:, None]
        b, s, d = x.shape
        xf = x.reshape(-1, d)
        gw = _wn(gate_v, gate_g)
        gates = jax.nn.softmax(xf @ gw.T + gate_b, axis=-1)
        top_k = min(2, E)
        _, top_idx = jax.lax.top_k(gates, top_k)
        out = jnp.zeros_like(xf)
        for i in range(E):
            mask = jnp.any(top_idx == i, axis=1).astype(xf.dtype)[:, None]
            xm = xf * mask
            W1 = _wn(w1_v[i], w1_g[i])
            h = xm @ W1.T + b1[i]
            h = h * jax.nn.sigmoid(h)
            W2 = _wn(w2_v[i], w2_g[i])
            out = out + mask * (h @ W2.T + b2[i])
        return out.reshape(b, s, d)

    def _L1_attn_ref(x, qK, qV, kK, kV, vK, vV, pK, pV, fK, fV):
        import jax, jax.numpy as jnp
        import numpy as np
        EMB = 128
        HEADS = 16
        EPS = 1e-05

        def layer_norm(x):
            mu = jnp.mean(x, axis=-1, keepdims=True)
            var = jnp.var(x, axis=-1, keepdims=True)
            return (x - mu) / jnp.sqrt(var + EPS)

        def pattention(x, K, V):
            scale = EMB ** (-0.5)
            a = jax.nn.softmax(scale * jnp.einsum('btc,nc->btn', x, K), axis=-1)
            return jnp.einsum('btn,nc->btc', a, V)

        def causal_sdpa(q, k, v):
            T = q.shape[2]
            d = q.shape[-1]
            scores = jnp.einsum('bhqd,bhkd->bhqk', q, k) / jnp.sqrt(jnp.asarray(d, q.dtype))
            mask = jnp.tril(jnp.ones((T, T), dtype=bool))
            scores = jnp.where(mask, scores, jnp.asarray(-jnp.inf, q.dtype))
            attn = jax.nn.softmax(scores, axis=-1)
            return jnp.einsum('bhqk,bhkd->bhqd', attn, v)
        B, T, C = x.shape
        H = HEADS
        D = C // H
        x_in = x
        h = layer_norm(x)
        k = pattention(h, kK, kV)
        q = pattention(h, qK, qV)
        v = pattention(h, vK, vV)
        to_heads = lambda t: t.reshape(B, T, H, D).transpose(0, 2, 1, 3)
        o = causal_sdpa(to_heads(q), to_heads(k), to_heads(v))
        o = o.transpose(0, 2, 1, 3).reshape(B, T, C)
        o = pattention(o, pK, pV)
        x = o + x_in
        x_inter = x
        x = pattention(layer_norm(x), fK, fV)
        return x + x_inter

    def _L1_ffn_ref(x, Wg, bg, W1, b1, W2, b2):
        import jax, jax.numpy as jnp
        import numpy as np
        DIM = 128
        NUM_EXPERTS = 6
        TOP_K = 2
        HIDDEN = DIM * 2
        gate_logits = jnp.einsum('bsd,de->bse', x, Wg) + bg
        topk_w, topk_idx = jax.lax.top_k(gate_logits, TOP_K)
        topk_w = jax.nn.softmax(topk_w, axis=-1)
        combine = jnp.sum(jax.nn.one_hot(topk_idx, NUM_EXPERTS, dtype=x.dtype) * topk_w[..., None], axis=-2)
        h = jnp.einsum('bsd,edh->ebsh', x, W1) + b1[:, None, None, :]
        h = jax.nn.gelu(h, approximate=False)
        y = jnp.einsum('ebsh,ehd->ebsd', h, W2) + b2[:, None, None, :]
        out = jnp.einsum('ebsd,bse->bsd', y, combine)
        return out

    def _L2_attn_ref(x, fw_in_w, fw_conv_w, fw_conv_b, fw_xproj_w, fw_dt_w, fw_dt_b, fw_Alog, fw_Dp, fw_out_w, bw_in_w, bw_conv_w, bw_conv_b, bw_xproj_w, bw_dt_w, bw_dt_b, bw_Alog, bw_Dp, bw_out_w, proj_w, proj_b, ln_w, ln_b):
        import jax, jax.numpy as jnp
        from jax import lax
        import numpy as np
        D_MODEL = 128
        D_STATE = 16
        D_CONV = 4
        EXPAND = 2
        D_INNER = EXPAND * D_MODEL
        DT_RANK = D_MODEL // 16
        B, L = (1, 128)

        def _mamba(x, in_w, conv_w, conv_b, xproj_w, dt_w, dt_b, Alog, Dp, out_w):
            xz = x @ in_w.T
            xi, z = jnp.split(xz, 2, axis=-1)
            xc = lax.conv_general_dilated(jnp.swapaxes(xi, 1, 2), conv_w, (1,), [(D_CONV - 1, 0)], feature_group_count=D_INNER)
            u = jnp.swapaxes(jax.nn.silu(xc + conv_b[None, :, None]), 1, 2)
            x_dbl = u @ xproj_w.T
            dt = x_dbl[..., :DT_RANK]
            Bm = x_dbl[..., DT_RANK:DT_RANK + D_STATE]
            Cm = x_dbl[..., DT_RANK + D_STATE:]
            delta = jax.nn.softplus(dt @ dt_w.T + dt_b)
            A = -jnp.exp(Alog)
            dA = jnp.exp(jnp.einsum('bld,dn->bldn', delta, A))
            dBu = jnp.einsum('bld,bln,bld->bldn', delta, Bm, u)

            def step(h, inputs):
                a, b, c = inputs
                h = a * h + b
                return (h, jnp.einsum('bdn,bn->bd', h, c))
            h0 = jnp.zeros((x.shape[0], D_INNER, D_STATE), x.dtype)
            _, ys = lax.scan(step, h0, (jnp.moveaxis(dA, 1, 0), jnp.moveaxis(dBu, 1, 0), jnp.moveaxis(Cm, 1, 0)))
            y = jnp.moveaxis(ys, 0, 1) + u * Dp
            return y * jax.nn.silu(z) @ out_w.T

        def _block(x, fw_in_w, fw_conv_w, fw_conv_b, fw_xproj_w, fw_dt_w, fw_dt_b, fw_Alog, fw_Dp, fw_out_w, bw_in_w, bw_conv_w, bw_conv_b, bw_xproj_w, bw_dt_w, bw_dt_b, bw_Alog, bw_Dp, bw_out_w, proj_w, proj_b, ln_w, ln_b):
            out_fw = _mamba(x, fw_in_w, fw_conv_w, fw_conv_b, fw_xproj_w, fw_dt_w, fw_dt_b, fw_Alog, fw_Dp, fw_out_w) + x
            xb = jnp.flip(x, axis=1)
            out_bw = jnp.flip(_mamba(xb, bw_in_w, bw_conv_w, bw_conv_b, bw_xproj_w, bw_dt_w, bw_dt_b, bw_Alog, bw_Dp, bw_out_w) + xb, axis=1)
            out = jnp.concatenate([out_fw, out_bw], axis=-1) @ proj_w.T + proj_b
            mu = out.mean(-1, keepdims=True)
            var = out.var(-1, keepdims=True)
            return (out - mu) / jnp.sqrt(var + 1e-05) * ln_w + ln_b
        return _block(x, fw_in_w, fw_conv_w, fw_conv_b, fw_xproj_w, fw_dt_w, fw_dt_b, fw_Alog, fw_Dp, fw_out_w, bw_in_w, bw_conv_w, bw_conv_b, bw_xproj_w, bw_dt_w, bw_dt_b, bw_Alog, bw_Dp, bw_out_w, proj_w, proj_b, ln_w, ln_b)

    def _L2_ffn_ref(x, gate_W, W1, b1, W2, b2, Ws1, bs1, Ws2, bs2, route_scale):
        import jax, jax.numpy as jnp
        import numpy as np
        B, S, D, E, H, K = (4, 256, 128, 8, 64, 2)
        scores = jax.nn.sigmoid(x @ gate_W) * route_scale
        topk_scores, topk_idx = jax.lax.top_k(scores, K)
        topk_w = topk_scores / topk_scores.sum(-1, keepdims=True)
        onehot = jax.nn.one_hot(topk_idx, E, dtype=x.dtype)
        gate_full = jnp.einsum('bsk,bske->bse', topk_w, onehot)
        h = jax.nn.gelu(jnp.einsum('bsd,edh->bseh', x, W1) + b1, approximate=False)
        y = jnp.einsum('bseh,ehd->bsed', h, W2) + b2
        expert_out = jnp.einsum('bse,bsed->bsd', gate_full, y)
        shared = jax.nn.gelu(x @ Ws1 + bs1, approximate=False) @ Ws2 + bs2
        return expert_out + shared

    def _L3_attn_ref(x, Wq, Wk, Wv):
        import jax, jax.numpy as jnp
        import numpy as np
        B, S, H, D = (4, 256, 128, 128)
        b, s, _ = x.shape
        d = Wq.shape[0]
        q = jnp.einsum('bsh,dh->bsd', x, Wq)
        k = jnp.einsum('bsh,dh->bsd', x, Wk)
        v = jnp.einsum('bsh,dh->bsd', x, Wv)
        kT = k.reshape(b, d, s)
        scores = jnp.matmul(q, kT) / jnp.sqrt(jnp.float32(d))
        attn = jax.nn.softmax(scores, axis=0)
        tril = jnp.tril(jnp.ones((s, s), dtype=bool))
        attn_masked = jnp.where(tril[None, :, :], attn, jnp.float32(1e-09))
        return jnp.matmul(attn_masked, v)

    def _L3_ffn_ref(x, gate_w, expert_bias, w_gate, w_up, w_down, shared_gate_w, shared_up_w, shared_down_w):
        import jax, jax.numpy as jnp
        import numpy as np
        B, S, D = (2, 64, 128)
        E, K, I = (16, 8, 128)
        I_SH = 128
        ROUTE_SCALE = 2.826
        gates = jnp.einsum('bsd,ed->bse', x, gate_w)
        scores = jax.nn.sigmoid(gates.astype(jnp.float32))
        sel_scores = scores + expert_bias
        _, inds = jax.lax.top_k(sel_scores, K)
        selected = jnp.take_along_axis(scores, inds, axis=-1)
        selected = selected / selected.sum(axis=-1, keepdims=True)
        selected = selected * ROUTE_SCALE
        onehot = jax.nn.one_hot(inds, E, dtype=selected.dtype)
        combine = jnp.einsum('bske,bsk->bse', onehot, selected)
        hg = jnp.einsum('bsd,eid->bsei', x, w_gate)
        hu = jnp.einsum('bsd,eid->bsei', x, w_up)
        h = jax.nn.silu(hg) * hu
        ye = jnp.einsum('bsei,edi->bsed', h, w_down)
        y = jnp.einsum('bsed,bse->bsd', ye, combine).astype(x.dtype)
        g = jnp.einsum('bsd,id->bsi', x, shared_gate_w)
        u = jnp.einsum('bsd,id->bsi', x, shared_up_w)
        y = y + jnp.einsum('bsi,di->bsd', jax.nn.silu(g) * u, shared_down_w)
        return y
    x = L0_attn_x
    x = x + _L0_attn_ref(_layernorm(x, axis=-1), L0_attn_Wq, L0_attn_Wk, L0_attn_Wv, L0_attn_memory, L0_attn_memory_norm, L0_attn_memory_weight)
    x = x + _L0_ffn_ref(_layernorm(x, axis=-1), L0_ffn_gate_v, L0_ffn_gate_g, L0_ffn_gate_b, L0_ffn_w1_v, L0_ffn_w1_g, L0_ffn_b1, L0_ffn_w2_v, L0_ffn_w2_g, L0_ffn_b2)
    x = x + _L1_attn_ref(_layernorm(x, axis=-1), L1_attn_qK, L1_attn_qV, L1_attn_kK, L1_attn_kV, L1_attn_vK, L1_attn_vV, L1_attn_pK, L1_attn_pV, L1_attn_fK, L1_attn_fV)
    x = x + _L1_ffn_ref(_layernorm(x, axis=-1), L1_ffn_Wg, L1_ffn_bg, L1_ffn_W1, L1_ffn_b1, L1_ffn_W2, L1_ffn_b2)
    x = x + _L2_attn_ref(_layernorm(x, axis=-1), L2_attn_fw_in_w, L2_attn_fw_conv_w, L2_attn_fw_conv_b, L2_attn_fw_xproj_w, L2_attn_fw_dt_w, L2_attn_fw_dt_b, L2_attn_fw_Alog, L2_attn_fw_Dp, L2_attn_fw_out_w, L2_attn_bw_in_w, L2_attn_bw_conv_w, L2_attn_bw_conv_b, L2_attn_bw_xproj_w, L2_attn_bw_dt_w, L2_attn_bw_dt_b, L2_attn_bw_Alog, L2_attn_bw_Dp, L2_attn_bw_out_w, L2_attn_proj_w, L2_attn_proj_b, L2_attn_ln_w, L2_attn_ln_b)
    x = x + _L2_ffn_ref(_layernorm(x, axis=-1), L2_ffn_gate_W, L2_ffn_W1, L2_ffn_b1, L2_ffn_W2, L2_ffn_b2, L2_ffn_Ws1, L2_ffn_bs1, L2_ffn_Ws2, L2_ffn_bs2, L2_ffn_route_scale)
    x = x + _L3_attn_ref(_layernorm(x, axis=-1), L3_attn_Wq, L3_attn_Wk, L3_attn_Wv)
    x = x + _L3_ffn_ref(_layernorm(x, axis=-1), L3_ffn_gate_w, L3_ffn_expert_bias, L3_ffn_w_gate, L3_ffn_w_up, L3_ffn_w_down, L3_ffn_shared_gate_w, L3_ffn_shared_up_w, L3_ffn_shared_down_w)
    return x

_drawn_inputs = setup_inputs


def setup_inputs(seed=0):
    import zlib

    import numpy as np

    out = dict(_drawn_inputs(seed))
    spreads = {'L0_attn_memory_norm': (1.0, 0.2),
     'L0_ffn_gate_g': (1.0, 0.535),
     'L0_ffn_gate_b': (0.0, 0.277),
     'L0_ffn_w1_g': (1.0, 0.2),
     'L0_ffn_b1': (0.0, 0.402),
     'L0_ffn_w2_g': (1.0, 0.595),
     'L0_ffn_b2': (0.0, 0.1),
     'L2_attn_fw_Dp': (1.0, 0.6),
     'L2_attn_bw_Dp': (1.0, 0.6),
     'L2_attn_proj_b': (0.0, 0.8),
     'L2_attn_ln_w': (1.0, 0.6),
     'L2_attn_ln_b': (0.0, 0.865),
     'L2_ffn_b1': (0.0, 2.0),
     'L2_ffn_b2': (0.0, 1.781),
     'L2_ffn_bs1': (0.0, 0.8),
     'L2_ffn_bs2': (0.0, 0.591),
     'L3_ffn_expert_bias': (0.0, 0.8)}
    factors = {'L0_attn_Wk': 5.694,
     'L0_attn_Wv': 4.814,
     'L1_attn_qK': 8.0,
     'L1_attn_qV': 8.0,
     'L1_attn_kK': 8.0,
     'L1_attn_kV': 8.0,
     'L1_attn_vK': 8.0,
     'L1_attn_vV': 8.0,
     'L1_attn_pK': 8.0,
     'L1_attn_fK': 8.0,
     'L1_attn_fV': 3.925,
     'L1_ffn_Wg': 8.0,
     'L1_ffn_bg': 8.0,
     'L1_ffn_W1': 8.0,
     'L1_ffn_b1': 8.0,
     'L1_ffn_W2': 5.774,
     'L1_ffn_b2': 27.002,
     'L2_attn_fw_in_w': 8.0,
     'L2_attn_fw_conv_w': 8.0,
     'L2_attn_fw_conv_b': 8.0,
     'L2_attn_fw_xproj_w': 8.0,
     'L2_attn_fw_dt_w': 8.0,
     'L2_attn_fw_dt_b': 64.0,
     'L2_attn_fw_Alog': 30.653,
     'L2_attn_fw_out_w': 8.0,
     'L2_attn_bw_in_w': 8.0,
     'L2_attn_bw_conv_w': 8.0,
     'L2_attn_bw_conv_b': 8.0,
     'L2_attn_bw_xproj_w': 8.0,
     'L2_attn_bw_dt_w': 8.0,
     'L2_attn_bw_dt_b': 64.0,
     'L2_attn_bw_Alog': 29.036,
     'L2_attn_bw_out_w': 8.0,
     'L2_ffn_gate_W': 8.0,
     'L2_ffn_W1': 8.0,
     'L2_ffn_W2': 8.0,
     'L2_ffn_Ws1': 8.0,
     'L2_ffn_Ws2': 8.0,
     'L3_ffn_gate_w': 8.0,
     'L3_ffn_w_gate': 8.0,
     'L3_ffn_w_up': 8.0,
     'L3_ffn_w_down': 8.0,
     'L3_ffn_shared_gate_w': 8.0,
     'L3_ffn_shared_up_w': 8.0,
     'L3_ffn_shared_down_w': 8.0}
    for name, (base, spread) in spreads.items():
        noise = np.random.default_rng([zlib.crc32(name.encode()), seed]).standard_normal(out[name].shape)
        drawn = base * np.exp(spread * noise) if base else spread * noise
        out[name] = jnp.asarray(drawn.astype(out[name].dtype))
    for name, factor in factors.items():
        out[name] = (out[name] * factor).astype(out[name].dtype)
    return out
```

```python
from contextlib import ExitStack

import concourse.bass as bass
from concourse import mybir

F32 = mybir.dt.float32
BF16 = mybir.dt.bfloat16
ALU = mybir.AluOpType
ACT = mybir.ActivationFunctionType
AX = mybir.AxisListType

P = 128
NB = 8
L = 512
T = NB * L
NT = T // P
TC = L // P
D = 128
SELW = 32
EPS = 1e-5


STAGES = ['a0', 'f0', 'a1', 'f1', 'a2', 'f2', 'a3', 'f3']


class State:
    pass


def chunk(c):
    return bass.ds(c * L, L)


class Chain:

    def __init__(self, eng, sem, base=0):
        self.eng, self.sem, self.value = eng, sem, base

    def __call__(self, ins):
        ins.then_inc(self.sem, 1)
        self.value = self.value + 1
        self.eng.wait_ge(self.sem, self.value)


def alone(eng, S):
    eng.sem_inc(S.passed, 1)


def stage_setup(nc, S, inp, fs):
    pending, clears = S.pending, S.clears
    S.pending, S.clears, S.n_cleared = [], [], len(clears)
    with nc.Block() as block:

        @block.sync
        def _(sp):
            sp.dma_start(S.x[:, :], inp["xT"]).then_inc(S.x_loaded, 16)
            if clears:
                sp.wait_ge(S.cleared, len(clears))
            for dst, src, sem in pending:
                sp.dma_start(dst, src).then_inc(sem, 16)
            sp.wait_ge(S.x_loaded, 16)

        @block.vector
        def _(dve):
            nc.vector.memset(S.ones[:, :], 1.0)
            nc.vector.memset(S.mean_w[:, :], 1.0 / D)
            nc.vector.memset(S.eps[:, :], EPS)
            dve.sem_inc(S.ln_centered, 4)
            dve.sem_inc(S.ln_normed, 4)
            dve.sem_inc(S.ln_var, 2)
            for sem, count in S.setup_primes + [p for f in fs.values() for p in f.primes]:
                dve.sem_inc(sem, count)

        @block.gpsimd
        def _(pool):
            for buf in clears:
                nc.gpsimd.memset(buf[:, :], 0.0).then_inc(S.cleared, 1)
            nc.gpsimd.memset(S.ident[:, :], 0.0).then_inc(S.setup_step, 1)
            pool.wait_ge(S.setup_step, 1)
            nc.gpsimd.affine_select(out=S.ident[:, :], in_=S.ident[:, :], compare_op=ALU.not_equal, fill=1.0,
                                    base=0, pattern=[[-1, P]], channel_multiplier=1).then_inc(S.setup_step, 1)


def build_selectors(nc, S, pool):
    nc.gpsimd.tensor_copy(S.ident_b[:, :], S.ident[:, :])
    nc.gpsimd.memset(S.sel[:, :, :], 0.0).then_inc(S.setup_step, 1)
    for part in range(3):
        pool.wait_ge(S.setup_step, 3 + part)
        nc.gpsimd.affine_select(out=S.sel[:, :, :], in_=S.sel[:, :, :], compare_op=ALU.not_equal, fill=1.0,
                                base=-SELW * part, pattern=[[-1, SELW], [0, P]],
                                channel_multiplier=1).then_inc(S.setup_step, 1)
    pool.wait_ge(S.setup_step, 6)
    for half in range(2):
        nc.gpsimd.tensor_copy(S.sel_pair[:, :, 64 * half:64 * half + 64],
                              S.sel[:, half:8:2, 64 * half:64 * half + 64])


def layer_norm(nc, S, src, dst, finish=None):
    call = S.ln_calls
    S.ln_calls += 1
    pending, clears, primes = S.pending, S.clears, S.primes
    S.pending, S.clears, S.primes = [], [], []
    S.n_cleared += len(clears)
    n_cleared = S.n_cleared
    base = NB * call
    with ExitStack() as ctx:
        sq = [ctx.enter_context(nc.sbuf_tensor(f"ln_sq{call}_{k}", [P, L], F32)) for k in range(2)]
        parts = ctx.enter_context(nc.sbuf_tensor(f"ln_parts{call}", [P, 96], F32))
        part = ctx.enter_context(nc.sbuf_tensor(f"ln_part{call}", [P, NT], BF16))
        rest = ctx.enter_context(nc.sbuf_tensor(f"ln_rest{call}", [P, NT], F32))
        rows = ctx.enter_context(nc.sbuf_tensor(f"ln_rows{call}", [96, P], BF16))
        std = ctx.enter_context(nc.sbuf_tensor(f"ln_std{call}", [P, NT], F32))
        v = ctx.enter_context(nc.sbuf_tensor(f"ln_v{call}", [P, NT], F32))
        rstd = ctx.enter_context(nc.sbuf_tensor(f"ln_rstd{call}", [P, NT], F32))
        mean = ctx.enter_context(nc.psum_tensor(f"ln_mean{call}", [P, 4, L], F32))
        spread = mean
        var = ctx.enter_context(nc.psum_tensor(f"ln_var{call}", [P, NT], F32))
        turned = ctx.enter_context(nc.psum_tensor(f"ln_turned{call}", [96, P], F32))
        block = ctx.enter_context(nc.Block())

        def slot(ring, c, n):
            return ring[:, bass.ds(c % n, 1), :].rearrange("p o n -> p (o n)")

        if pending:
            @block.sync
            def _(sp):
                if clears:
                    sp.wait_ge(S.cleared, n_cleared)
                for to, what, sem in pending:
                    sp.dma_start(to, what).then_inc(sem, 16)

        @block.tensor
        def _(pe):
            def means(i):
                for k in range(2):
                    c = 2 * i + k
                    pe.wait_ge(S.ln_centered, base + c + 1)
                    nc.tensor.matmul(slot(mean, c, 4), S.mean_w[:, :], src[:, chunk(c)],
                                     start=True, stop=True).then_inc(S.ln_mean, 1)

            def variances(i):
                for k in range(2):
                    c = 2 * i + k
                    pe.wait_ge(S.ln_squared, base + c + 1)
                    for t in range(TC):
                        last = nc.tensor.matmul(var[:, bass.ds(c * TC + t, 1)], sq[k][:, t * P:(t + 1) * P],
                                                S.mean_w[:, 0:1], start=True, stop=True)
                    last.then_inc(S.ln_var, 1)

            means(0)
            means(1)
            with pe.Fori(0, NB // 2 - 2) as i:
                variances(i)
                means(i + 2)
            variances(NB // 2 - 2)
            variances(NB // 2 - 1)
            pe.wait_ge(S.ln_rstd, call + 1)
            nc.tensor.transpose(turned[:, :], parts[:, :], S.ident[:, :]).then_inc(S.ln_turned, 1)
            pe.wait_ge(S.setup_step, 6)
            pe.wait_ge(S.ln_rows, call + 1)
            for c in range(NB):
                pe.wait_ge(S.ln_normed, base + c + 1)
                for t in range(TC):
                    last = nc.tensor.matmul(spread[:, c % 4, t * P:(t + 1) * P], S.sel[:, c * TC + t, :],
                                            rows[:, :], start=True, stop=True)
                last.then_inc(S.ln_spread, 1)

        @block.vector
        def _(dve):
            for sem, count in primes:
                dve.sem_inc(sem, count)
            with dve.Fori(0, NB) as c:
                dve.wait_ge(S.ln_mean, base + c + 1)
                nc.vector.tensor_tensor(dst[:, chunk(c)], src[:, chunk(c)], slot(mean, c, 4),
                                        ALU.subtract).then_inc(S.ln_centered, 1)
            dve.wait_ge(S.ln_std, call + 1)
            chain = Chain(dve, S.ln_step, 8 * call)
            nc.vector.tensor_scalar(v[:, :], var[:, :], EPS, None, ALU.add)
            chain(nc.vector.reciprocal(rstd[:, :], std[:, :]))
            chain(nc.vector.tensor_tensor(v[:, :], v[:, :], rstd[:, :], ALU.mult))
            chain(nc.vector.tensor_tensor(v[:, :], v[:, :], rstd[:, :], ALU.mult))
            chain(nc.vector.tensor_scalar(v[:, :], v[:, :], -0.5, 1.5, ALU.mult, ALU.add))
            chain(nc.vector.tensor_tensor(rstd[:, :], rstd[:, :], v[:, :], ALU.mult))
            chain(nc.vector.tensor_copy(part[:, :], rstd[:, :]))
            nc.vector.tensor_copy(parts[:, 0:NT], part[:, :])
            chain(nc.vector.tensor_tensor(rest[:, :], rstd[:, :], part[:, :], ALU.subtract))
            chain(nc.vector.tensor_copy(part[:, :], rest[:, :]))
            nc.vector.tensor_copy(parts[:, SELW:SELW + NT], part[:, :])
            nc.vector.tensor_tensor(parts[:, 2 * SELW:2 * SELW + NT], rest[:, :], part[:, :],
                                    ALU.subtract).then_inc(S.ln_rstd, 1)
            dve.wait_ge(S.ln_turned, call + 1)
            nc.vector.tensor_copy(rows[:, :], turned[:, :]).then_inc(S.ln_rows, 1)
            with dve.Fori(0, NB) as c:
                dve.wait_ge(S.ln_spread, base + c + 1)
                nc.vector.tensor_tensor(dst[:, chunk(c)], dst[:, chunk(c)], slot(spread, c, 4),
                                        ALU.mult).then_inc(S.ln_normed, 1)
                if finish is not None:
                    dve.wait_ge(S.ln_normed, base + c + 5)
                    finish(dve, c)

        @block.scalar
        def _(act):
            with act.Fori(0, NB // 2) as i:
                for k in range(2):
                    c = 2 * i + k
                    act.wait_ge(S.ln_centered, base + c + 5)
                    act.wait_ge(S.ln_var, base + c + 1)
                    nc.scalar.activation(sq[k][:, :], dst[:, chunk(c)], ACT.Square).then_inc(S.ln_squared, 1)
            act.wait_ge(S.ln_var, base + NB + 2)
            nc.scalar.activation(std[:, :], var[:, :], ACT.Sqrt, bias=S.eps[:, 0:1]).then_inc(S.ln_std, 1)

        @block.gpsimd
        def _(pool):
            for buf in clears:
                nc.gpsimd.memset(buf[:, :], 0.0).then_inc(S.cleared, 1)
            if call == 0:
                build_selectors(nc, S, pool)


def gates(nc, S, f, h):
    E, EG, K, kind = f.E, f.EG, f.K, f.kind
    with ExitStack() as ctx:
        def sb(name, shape, dt=F32):
            return ctx.enter_context(nc.sbuf_tensor(f"{f.name}_{name}", shape, dt))

        def ps(name, shape):
            return ctx.enter_context(nc.psum_tensor(f"{f.name}_{name}", shape, F32))

        logits = ps("logits", [P, NT, E])
        turned = ps("turned", [96, 2, TC, P])
        lg = sb("lg", [P, NT, E])
        score = sb("score", [P, NT, E])
        key = sb("key", [P, NT, E])
        beats = sb("beats", [P, NT, E, E], BF16)
        rank = sb("rank", [P, NT, E])
        picked = sb("picked", [P, NT, E])
        top = sb("top", [P, NT])
        total = sb("total", [P, NT])
        gate = sb("gate", [P, NT, EG])
        rest = sb("rest", [P, NT, EG])
        part = sb("part", [P, NT, EG], BF16)
        parts = sb("parts", [P, NT, 96])
        block = ctx.enter_context(nc.Block())

        def wide(col):
            return col[:, :].rearrange("p (t o) -> p t o", o=1).to_broadcast([P, NT, E])

        def rows(vec):
            return vec.rearrange("p (o e) -> p o e", o=1).to_broadcast([P, NT, E])

        @block.tensor
        def _(pe):
            pe.wait_ge(f.loaded, 16 * f.n_loads)
            if f.kind == "mask":
                pe.wait_ge(f.prep_done, 2)
            for t in range(NT):
                last = nc.tensor.matmul(logits[:, t, :], h[:, t * P:(t + 1) * P], f.router, start=True, stop=True)
            last.then_inc(f.logits_done, 1)
            pe.wait_ge(f.parts_done, 1)
            for c in range(NB):
                if c >= 2:
                    pe.wait_ge(f.turned_copied, c - 1)
                    if f.b2 is not None:
                        pe.wait_ge(f.turned_copied_f, c - 1)
                for t in range(TC):
                    last = nc.tensor.transpose(turned[:, c % 2, t, :], parts[:, c * TC + t, :], S.ident[:, :])
                last.then_inc(f.turned_done, 1)

        @block.scalar
        def _(act):
            if kind in ("sigmoid", "sigmoid_bias"):
                act.wait_ge(f.logits_done, 1)
                nc.scalar.activation(score[:, :, :], logits[:, :, :], ACT.Sigmoid).then_inc(f.score_done, 1)
            if kind == "softmax":
                act.wait_ge(f.shifted_done, 1)
                nc.scalar.activation(score[:, :, :], score[:, :, :], ACT.Exp).then_inc(f.score_done, 1)
            for c in range(NB):
                act.wait_ge(f.turned_done, c + 1)
                nc.scalar.activation(f.gates_b[:, c * L:(c + 1) * L],
                                     turned[:, c % 2, :, :].rearrange("p t n -> p (t n)"),
                                     ACT.Copy).then_inc(f.turned_copied, 1)

        @block.gpsimd
        def _(pool):
            nc.gpsimd.memset(parts[:, :, :], 0.0).then_inc(f.parts_cleared, 1)

        @block.vector
        def _(dve):
            step = Chain(dve, f.step, f.prep_steps)
            step(nc.vector.memset(beats[:, :, :, :], 0.0))
            if EG > E:
                step(nc.vector.memset(gate[:, :, E:EG], 1.0))
            dve.wait_ge(f.logits_done, 1)
            if kind in ("mask", "softmax"):
                step(nc.vector.tensor_tensor(key[:, :, :], logits[:, :, :], rows(f.router_bias), ALU.add))
            elif kind == "sigmoid":
                dve.wait_ge(f.score_done, 1)
                step(nc.vector.tensor_scalar(key[:, :, :], logits[:, :, :], f.route_scale, None, ALU.mult))
            else:
                dve.wait_ge(f.score_done, 1)
                step(nc.vector.tensor_tensor(key[:, :, :], score[:, :, :], rows(f.router_bias), ALU.add))
            for e in range(E):
                for lo, hi, op in ((0, e, ALU.is_ge), (e + 1, E, ALU.is_gt)):
                    if hi > lo:
                        last = nc.vector.tensor_tensor(beats[:, :, e, lo:hi], key[:, :, lo:hi],
                                                       key[:, :, e:e + 1].to_broadcast([P, NT, hi - lo]), op)
            step(last)
            step(nc.vector.tensor_reduce(rank[:, :, :], beats[:, :, :, :], AX.X, ALU.add))
            if kind == "mask":
                step(nc.vector.tensor_scalar(gate[:, :, 0:E], rank[:, :, :], float(K), None, ALU.is_lt))
            else:
                step(nc.vector.tensor_scalar(picked[:, :, :], rank[:, :, :], float(K), None, ALU.is_lt))
                if kind == "softmax":
                    step(nc.vector.tensor_reduce(top[:, :], key[:, :, :], AX.X, ALU.max))
                    nc.vector.tensor_tensor(score[:, :, :], key[:, :, :], wide(top),
                                            ALU.subtract).then_inc(f.shifted_done, 1)
                dve.wait_ge(f.score_done, 1)
                step(nc.vector.tensor_tensor(picked[:, :, :], picked[:, :, :], score[:, :, :], ALU.mult))
                if kind == "sigmoid":
                    step(nc.vector.tensor_scalar(picked[:, :, :], picked[:, :, :], f.route_scale, None, ALU.mult))
                step(nc.vector.tensor_reduce(total[:, :], picked[:, :, :], AX.X, ALU.add))
                step(nc.vector.reciprocal(total[:, :], total[:, :]))
                step(nc.vector.tensor_tensor(gate[:, :, 0:E], picked[:, :, :], wide(total), ALU.mult))
                if f.factor != 1.0:
                    step(nc.vector.tensor_scalar(gate[:, :, 0:E], gate[:, :, 0:E], f.factor, None, ALU.mult))
            dve.wait_ge(f.parts_cleared, 1)
            step(nc.vector.tensor_copy(part[:, :, :], gate[:, :, :]))
            nc.vector.tensor_copy(parts[:, :, 0:EG], part[:, :, :])
            step(nc.vector.tensor_tensor(rest[:, :, :], gate[:, :, :], part[:, :, :], ALU.subtract))
            step(nc.vector.tensor_copy(part[:, :, :], rest[:, :, :]))
            nc.vector.tensor_copy(parts[:, :, SELW:SELW + EG], part[:, :, :])
            nc.vector.tensor_tensor(parts[:, :, 2 * SELW:2 * SELW + EG], rest[:, :, :], part[:, :, :],
                                    ALU.subtract).then_inc(f.parts_done, 1)
            if f.b2 is not None:
                for c in range(NB):
                    dve.wait_ge(f.turned_copied, c + 1)
                    nc.vector.tensor_copy(f.gates_f[:, c * L:(c + 1) * L],
                                          turned[:, c % 2, :, :].rearrange("p t n -> p (t n)")
                                          ).then_inc(f.turned_copied_f, 1)


def experts(nc, S, f, h):
    U, R, LAG = len(f.units), 4, 2
    gated = f.units[0].up is not None
    HR = 2 if gated else 4
    groups = []
    for u, unit in enumerate(f.units):
        if not groups or f.units[groups[-1][0]].gate_key != unit.gate_key:
            groups.append([])
        groups[-1].append(u)
    G = len(groups)
    group_of = {u: g for g, us in enumerate(groups) for u in us}
    with ExitStack() as ctx:
        hid = ctx.enter_context(nc.psum_tensor(f"{f.name}_hid", [P, 4, L], F32))
        spread = ctx.enter_context(nc.psum_tensor(f"{f.name}_spread", [P, 2, L], F32))
        y = ctx.enter_context(nc.psum_tensor(f"{f.name}_y", [P, L], F32))
        a = ctx.enter_context(nc.sbuf_tensor(f"{f.name}_a", [P, R, L], F32))
        s = ctx.enter_context(nc.sbuf_tensor(f"{f.name}_s", [P, R, L], F32))
        m = ctx.enter_context(nc.sbuf_tensor(f"{f.name}_m", [P, R, L], F32)) if gated else None
        block = ctx.enter_context(nc.Block())

        def prior(u, ring):
            return u - ring + U + 1 if u >= ring else max(v for v in range(U) if v % ring == u) + 1

        def prior_group(g):
            v = g - 2 + G if g >= 2 else max(w for w in range(G) if w % 2 == g)
            return (groups[v % G][-1] + 1) + (U if g >= 2 else 0)

        free = f.multiplied if gated else f.activated

        @block.tensor
        def _(pe):
            with pe.Fori(0, NB) as c:
                for step in range(U + LAG):
                    if step < U:
                        u, unit = step, f.units[step]
                        pe.wait_ge(free, U * c + prior(u, HR))
                        if gated:
                            nc.tensor.matmul(hid[:, 2 * (u % 2), :], unit.w1, h[:, chunk(c)], start=True, stop=True)
                            last = nc.tensor.matmul(hid[:, 2 * (u % 2) + 1, :], unit.up, h[:, chunk(c)],
                                                    start=True, stop=True)
                        else:
                            last = nc.tensor.matmul(hid[:, u % 4, :], unit.w1, h[:, chunk(c)], start=True, stop=True)
                        last.then_inc(f.hidden, 1)
                    if step >= LAG:
                        u, unit = step - LAG, f.units[step - LAG]
                        if u == 0:
                            pe.wait_ge(f.added, c + 1)
                        pe.wait_ge(f.scaled, U * c + U + u + 1)
                        nc.tensor.matmul(y[:, :], unit.w2, s[:, u % R, :], start=(u == 0),
                                         stop=(u == U - 1 and f.b2 is None)).then_inc(f.used, 1)
                    if step < U and groups[group_of[step]][0] == step:
                        g = group_of[step]
                        pe.wait_ge(f.scaled, U * c + prior_group(g))
                        nc.tensor.matmul(spread[:, g % 2, :], f.units[step].gate, f.gates_b[:, chunk(c)],
                                         start=True, stop=True).then_inc(f.spread_done, 1)
                if f.b2 is not None:
                    nc.tensor.matmul(y[:, :], f.b2, f.gates_f[:, chunk(c)], start=False,
                                     stop=True).then_inc(f.summed, 1)

        @block.scalar
        def _(act):
            with act.Fori(0, NB) as c:
                for u, unit in enumerate(f.units):
                    act.wait_ge(f.hidden, U * c + u + 1)
                    act.wait_ge(f.scaled, U * c + prior(u, R))
                    slot = 2 * (u % 2) if gated else u % 4
                    nc.scalar.activation(a[:, u % R, :], hid[:, slot, :], f.func,
                                         bias=unit.bias if unit.bias is not None else 0.0,
                                         scale=unit.scale if unit.scale is not None else 1.0).then_inc(f.activated, 1)

        @block.vector
        def _(dve):
            def scale(c, u):
                g = group_of[u]
                if groups[g][0] == u:
                    dve.wait_ge(f.spread_done, G * c + g + 1)
                if gated:
                    dve.wait_ge(f.multiplied, U * c + U + u + 1)
                else:
                    dve.wait_ge(f.activated, U * c + U + u + 1)
                dve.wait_ge(f.used, U * c + prior(u, R))
                nc.vector.tensor_tensor(s[:, u % R, :], (m if gated else a)[:, u % R, :], spread[:, g % 2, :],
                                        ALU.mult).then_inc(f.scaled, 1)

            with dve.Fori(0, NB) as c:
                for u in range(U):
                    if gated:
                        dve.wait_ge(f.activated, U * c + U + u + 1)
                        nc.vector.tensor_tensor(m[:, u % R, :], a[:, u % R, :], hid[:, 2 * (u % 2) + 1, :],
                                                ALU.mult).then_inc(f.multiplied, 1)
                        if u >= 1:
                            scale(c, u - 1)
                    else:
                        scale(c, u)
                if gated:
                    scale(c, U - 1)
                if f.b2 is not None:
                    dve.wait_ge(f.summed, c + 1)
                else:
                    dve.wait_ge(f.used, U * c + 2 * U)
                nc.vector.tensor_tensor(S.x[:, chunk(c)], S.x[:, chunk(c)], y[:, :], ALU.add).then_inc(f.added, 1)


def normalise_weights(nc, S, f):
    E, HT = f.E, 4
    with ExitStack() as ctx:
        sq = [ctx.enter_context(nc.sbuf_tensor(f"wn_sq{k}", [P, L], F32)) for k in range(2)]
        norm1 = ctx.enter_context(nc.sbuf_tensor("wn_norm1", [P, E * HT], F32))
        norm2 = ctx.enter_context(nc.sbuf_tensor("wn_norm2", [P, E * D], F32))
        normr = ctx.enter_context(nc.sbuf_tensor("wn_normr", [P, E], F32))
        ss1 = ctx.enter_context(nc.psum_tensor("wn_ss1", [P, L], F32))
        ss2 = ctx.enter_context(nc.psum_tensor("wn_ss2", [P, E * D], F32))
        ssr = ctx.enter_context(nc.psum_tensor("wn_ssr", [P, L], F32))
        block = ctx.enter_context(nc.Block())
        jobs = [f.w1[:, j * L:(j + 1) * L] for j in range(E)] + [f.w2[:, j * L:(j + 1) * L] for j in range(E)]

        @block.scalar
        def _(act):
            act.wait_ge(f.loaded, 16 * f.n_loads)
            for n, w in enumerate(jobs + [f.router]):
                if n >= 2:
                    act.wait_ge(f.wn_summed, n - 1)
                nc.scalar.activation(sq[n % 2][:, 0:w.shape[1]], w, ACT.Square).then_inc(f.wn_squared, 1)
            act.wait_ge(f.wn_summed, 2 * E + 1)
            nc.scalar.activation(norm1[:, :], ss1[:, 0:E * HT], ACT.Sqrt).then_inc(f.wn_rooted, 1)
            nc.scalar.activation(norm2[:, :], ss2[:, :], ACT.Sqrt).then_inc(f.wn_rooted, 1)
            nc.scalar.activation(normr[:, :], ssr[:, 0:E], ACT.Sqrt).then_inc(f.wn_rooted, 1)

        @block.tensor
        def _(pe):
            for n in range(2 * E + 1):
                pe.wait_ge(f.wn_squared, n + 1)
                if n < E:
                    for t in range(HT):
                        last = nc.tensor.matmul(ss1[:, n * HT + t:n * HT + t + 1], sq[n % 2][:, t * P:(t + 1) * P],
                                                S.ones[:, 0:1], start=True, stop=True)
                elif n < 2 * E:
                    e = n - E
                    for t in range(HT):
                        last = nc.tensor.matmul(ss2[:, e * D:(e + 1) * D], S.ones[:, :],
                                                sq[n % 2][:, t * D:(t + 1) * D], start=(t == 0), stop=(t == HT - 1))
                else:
                    last = nc.tensor.matmul(ssr[:, 0:E], S.ones[:, :], sq[n % 2][:, 0:E], start=True, stop=True)
                last.then_inc(f.wn_summed, 1)

        @block.vector
        def _(dve):
            step = Chain(dve, f.step)
            dve.wait_ge(f.wn_rooted, 3)
            for norm, gain in ((norm1, f.g1), (norm2, f.g2), (normr, f.router_gain)):
                step(nc.vector.tensor_scalar(norm[:, :], norm[:, :], 1e-12, None, ALU.max))
                step(nc.vector.reciprocal(norm[:, :], norm[:, :]))
                step(nc.vector.tensor_tensor(norm[:, :], norm[:, :], gain, ALU.mult))
            assert step.value == f.prep_steps - 1
            step(nc.vector.tensor_copy(f.scale1[:, :], norm1[:, :]))
            nc.vector.tensor_tensor(f.router, f.router, normr[:, :], ALU.mult).then_inc(f.prep_done, 1)
            w2 = f.w2[:, :].rearrange("p (e t d) -> p e t d", e=E, t=HT)
            nc.vector.tensor_tensor(w2, w2, norm2[:, :].rearrange("p (e o d) -> p e o d", e=E, o=1)
                                    .to_broadcast([P, E, HT, D]), ALU.mult).then_inc(f.prep_done, 1)


H, DH = 16, 8
ROWS = 9 * DH
MASKED = -1e30
PV_AT = (1, 2)


class Attention:
    pass


def new_attention(nc, S, name, KVH, causal):
    a = Attention()
    a.name, a.KVH, a.causal = name, KVH, causal
    a.scale = float(DH) ** -0.5
    a.q_rows = nc.dram_tensor(f"{name}_q_rows", (H, ROWS, T), BF16).ap()
    a.k_rows = nc.dram_tensor(f"{name}_k_rows", (KVH, ROWS, T), BF16).ap()
    a.v = nc.dram_tensor(f"{name}_v_rows", (T, KVH * DH), F32).ap()
    a.max_rows = nc.dram_tensor(f"{name}_max_rows", (2, 3, H * L), BF16).ap()
    a.pv = nc.dram_tensor(f"{name}_pv_rows", (NB, 4, P, L), F32).ap()
    return a


def attention_semaphores(S):
    s, sem = State(), S.sem
    s.calls = 0
    s.stack = [[sem(f"at_stack{k}{g}") for g in range(4)] for k in range(2)]
    s.v_loaded = [sem("at_v0"), sem("at_v1")]
    s.ready = sem("at_ready")
    s.v_ready = sem("at_v_ready")
    s.scored = sem("at_scored")
    s.maxed = sem("at_maxed")
    s.max_turned = sem("at_max_turned")
    s.max_parts = sem("at_max_parts")
    s.max_step = sem("at_max_step")
    s.max_stored = sem("at_max_stored")
    s.max_loaded = [sem("at_max_l0"), sem("at_max_l1")]
    s.st_done = sem("at_st_done")
    s.exp_done = sem("at_exp_done")
    s.pv_done = sem("at_pv_done")
    s.evacuated = sem("at_evacuated")
    s.pv_stored = [sem("at_pv_s0"), sem("at_pv_s1")]
    s.step = sem("at_step")
    S.at = s
    S.setup_primes += [(s.maxed, 2), (s.exp_done, 2), (s.pv_done, 2), (s.evacuated, 2)]


def attend(nc, S, a):
    s, KVH, HK = S.at, a.KVH, H // a.KVH
    call = s.calls
    s.calls += 1
    with ExitStack() as ctx:
        def sb(name, shape, dt=F32):
            return ctx.enter_context(nc.sbuf_tensor(f"{a.name}_{name}", shape, dt))

        def ps(name, shape):
            return ctx.enter_context(nc.psum_tensor(f"{a.name}_{name}", shape, F32))

        q = [sb(f"q{k}", [ROWS + 3, H, L], BF16) for k in range(2)]
        kk = [sb(f"k{k}", [ROWS + 3, KVH, L], BF16) for k in range(2)]
        v_in = [sb(f"v_in{k}", [P, TC, KVH * DH]) for k in range(2)]
        v = [sb(f"v{k}", [P, TC, KVH, 32]) for k in range(2)]
        prob = [sb(f"prob{k}", [P, 4, 2 * L]) for k in range(2)]
        top = sb("top", [P, TC, H])
        max_rest = sb("max_rest", [H, L])
        max_part = sb("max_part", [H, 3, L], BF16)
        pv_sb = [sb(f"pv_sb{k}", [P, L]) for k in range(2)]
        if a.causal:
            mask_q = sb("mask_q", [P, P], BF16)
            mask_k = sb("mask_k", [P, P], BF16)
        st = ps("st", [P, 2, 2 * L])
        sc = ps("sc", [P, 2, L])
        pv = ps("pv", [P, 2, L])
        block = ctx.enter_context(nc.Block())

        if a.causal:
            SPAN = [[(0, 0, L), (L, P, L - P)], [(0, 2 * P, 2 * P), (2 * P, 3 * P, P)]]
        else:
            SPAN = [[(0, 0, L), (L, 0, L)]] * 2

        def width(kp):
            return sum(w for _, _, w in SPAN[kp])

        def steps(eng, body):
            body(0, True, False, False, 0)
            body(1, True, False, True, 1)
            with eng.Fori(1, NB // 2) as i:
                for k in range(2):
                    body(2 * i + k, True, True, True, k)
            body(NB, False, True, True, 0)
            body(NB + 1, False, True, False, 1)

        def waves(b, B1, B2):
            for w in range(8):
                if w < 2:
                    yield w, (b - 2 if B1 else None), w + 6, 0
                else:
                    yield w, (b - 1 if B2 else None), w - 2, 1

        nB = call * NB

        @block.sync
        def _(sp):
            sp.wait_ge(s.ready, 4 * call + 4)

            def load(b, g, k, first=False):
                if not first:
                    sp.wait_ge(s.st_done, (nB + b - 2) * 32 + 8 * g + 8)
                alone(sp, S)
                sp.dma_start(q[k][0:ROWS, 4 * g:4 * g + 4, :],
                             a.q_rows[4 * g:4 * g + 4, :, chunk(b)].rearrange("h r n -> r h n")).then_inc(s.stack[k][g], 16)
                n = 4 // HK
                sp.dma_start(kk[k][0:ROWS, n * g:n * g + n, :],
                             a.k_rows[n * g:n * g + n, :, chunk(b)].rearrange("h r n -> r h n")).then_inc(s.stack[k][g], 16)

            def store(b, g):
                sp.wait_ge(s.evacuated, (nB + b) * 4 + g + 3)
                alone(sp, S)
                sp.dma_start(a.pv[bass.ds(b, 1), g].rearrange("o p n -> (o p) n"),
                             pv_sb[g % 2][:, :]).then_inc(s.pv_stored[g % 2], 16)

            def load_v(b, k, first=False):
                if not first:
                    sp.wait_ge(s.v_ready, nB + b - 1)
                alone(sp, S)
                sp.dma_start(v_in[k][:, :, :], a.v[chunk(b), :].rearrange("(t p) c -> p t c", p=P)
                             ).then_inc(s.v_loaded[k], 16)

            def body(b, A, B1, B2, k):
                early = isinstance(b, int) and b < 2
                if A and not (isinstance(b, int) and b == 0):
                    load(b, 3, k, first=early)
                if B1:
                    store(b - 2, 3)
                more = A and not (isinstance(b, int) and b >= NB)
                for g in range(3):
                    if more:
                        load_next(b, g, k, early)
                    if B2:
                        store(b - 1, g)

            def load_next(b, g, k, early):
                first = isinstance(b, int) and b == 0
                load(b + 1, g, 1 - k, first=first)
                if g == 0:
                    load_v(b + 1, 1 - k, first=first)

            for g in range(4):
                load(0, g, 0, first=True)
            load_v(0, 0, first=True)
            body(0, True, False, False, 0)
            body(1, True, False, True, 1)
            with sp.Fori(1, NB // 2 - 1) as i:
                for k in range(2):
                    body(2 * i + k, True, True, True, k)
            body(NB - 2, True, True, True, 0)
            load(NB - 1, 3, 1)
            store(NB - 3, 3)
            for g in range(3):
                store(NB - 2, g)
            store(NB - 2, 3)
            for g in range(4):
                store(NB - 1, g)
            for k in range(2):
                sp.wait_ge(s.pv_stored[k], 16 * 2 * (nB + NB))

        @block.gpsimd
        def _(pool):
            for k in range(2):
                nc.gpsimd.memset(v[k][:, :, :, :], 0.0).then_inc(s.ready, 1)
            pool.wait_ge(s.ready, 4 * call + 4)
            for k in range(2):
                nc.gpsimd.memset(v[k][:, :, :, DH:DH + 1], 1.0).then_inc(s.step, 1)
            if a.causal:
                nc.gpsimd.memset(mask_q[:, :], 0.0).then_inc(s.step, 1)
                nc.gpsimd.memset(mask_k[:, :], 0.0).then_inc(s.step, 1)
                pool.wait_ge(s.step, 2 * call + 4)
                nc.gpsimd.affine_select(out=mask_q[:, :], in_=mask_q[:, :], compare_op=ALU.is_ge, fill=MASKED,
                                        base=0, pattern=[[-1, P]], channel_multiplier=1).then_inc(s.step, 1)
                nc.gpsimd.affine_select(out=mask_k[:, :], in_=mask_k[:, :], compare_op=ALU.is_ge, fill=MASKED,
                                        base=0, pattern=[[1, P]], channel_multiplier=-1).then_inc(s.step, 1)

            def body(b, A, B1, B2, k):
                if not A:
                    return
                pool.wait_ge(s.v_loaded[k], 16 * ((nB + b) // 2 + 1) if isinstance(b, int)
                             else 16 * (nB // 2) + 8 * (b - k) + 16)
                if not (isinstance(b, int) and b < 2):
                    pool.wait_ge(s.pv_done, (nB + b) * 8 - 6)
                alone(pool, S)
                nc.gpsimd.tensor_copy(v[k][:, :, :, 0:DH], v_in[k][:, :, :].rearrange("p t (h d) -> p t h d", d=DH)
                                      ).then_inc(s.v_ready, 1)
                pool.wait_ge(s.max_parts, nB + b + 1)
                alone(pool, S)
                nc.gpsimd.dma_start(a.max_rows[k].rearrange("i (h n) -> h i n", h=H), max_part[:, :, :]
                                    ).then_inc(s.max_stored, 16)
                pool.wait_ge(s.max_stored, 16 * (nB + b) + 16)
                alone(pool, S)
                nc.gpsimd.dma_start(q[k][ROWS:ROWS + 3, :, :].rearrange("r h n -> r (h n)"), a.max_rows[k]
                                    ).then_inc(s.max_loaded[k], 16)

            steps(pool, body)

        @block.tensor
        def _(pe):
            pe.wait_ge(s.ready, 4 * call + 4)
            pe.wait_ge(s.step, 2 + 6 * call if not a.causal else 2 * call + 6)

            def score_tile(b, n, t, k):
                pe.wait_ge(s.maxed, (nB + b) * 64 + 4 * n + t + 1)
                if t == 0 and n == 0 and not (isinstance(b, int) and b == 0 and call == 0):
                    pe.wait_ge(s.max_parts, nB + b)
                if n % 4 == 0 and t == 0:
                    pe.wait_ge(s.stack[k][n // 4], 32 * ((nB + b) // 2 + 1) if isinstance(b, int)
                               else 16 * nB + 16 * (b - k) + 32)
                w = (t + 1) * P if a.causal else L
                last = nc.tensor.matmul(sc[:, t % 2, 0:w], q[k][0:ROWS, n, t * P:(t + 1) * P], kk[k][0:ROWS, n // HK, 0:w],
                                        start=True, stop=not a.causal)
                if a.causal:
                    last = nc.tensor.matmul(sc[:, t % 2, t * P:w], S.ident_b[:, :], mask_q[:, :], start=False, stop=True)
                last.then_inc(s.scored, 1)

            def scores_of_keys(bb, w, j, k):
                g, kp = w // 2, w % 2
                n = 4 * g + j
                if w == 0 and j == 0:
                    pe.wait_ge(s.max_loaded[k], 16 * ((nB + bb) // 2 + 1) if isinstance(bb, int)
                               else 8 * nB + 8 * (bb - k) + 16)
                pe.wait_ge(s.exp_done, (nB + bb) * 32 + 4 * w + j + 1)
                for kt in range(2):
                    col, first, wide = SPAN[kp][kt]
                    key = (2 * kp + kt) * P
                    last = nc.tensor.matmul(st[:, j % 2, col:col + wide], kk[k][:, n // HK, key:key + P],
                                            q[k][:, n, first:first + wide], start=True, stop=not a.causal)
                    if a.causal:
                        last = nc.tensor.matmul(st[:, j % 2, col:col + P], S.ident_b[:, :], mask_k[:, :],
                                                start=False, stop=True)
                last.then_inc(s.st_done, 1)

            def products(bb, w, k, kt):
                g, kp = w // 2, w % 2
                if kt == 0:
                    pe.wait_ge(s.exp_done, (nB + bb) * 32 + 4 * w + 4 + 2)
                if kp == 0 and kt == 0:
                    pe.wait_ge(s.evacuated, (nB + bb) * 4 + g + 1)
                if w == 0 and kt == 0:
                    pe.wait_ge(s.v_ready, nB + bb + 1)
                col, first, wide = SPAN[kp][kt]
                for j in range(4):
                    last = nc.tensor.matmul(pv[32 * j:32 * j + 32, g % 2, first:L],
                                                v[k][:, 2 * kp + kt, (4 * g + j) // HK, :],
                                                prob[w % 2][:, j, col:col + wide], start=(kp == 0 and kt == 0),
                                                stop=(kp == 1 and kt == 1), tile_position=(0, 32 * j),
                                                skip_group_check=True)
                if kt == 1:
                    last.then_inc(s.pv_done, 1)

            def body(b, A, B1, B2, k):
                for w, bb, wb, odd in waves(b, B1, B2):
                    kb = k ^ odd
                    for j in range(4):
                        if bb is not None:
                            scores_of_keys(bb, wb, j, kb)
                        if A:
                            score_tile(b, 2 * w + j // 2, 2 * j % 4, k)
                        if j in PV_AT:
                            kt = PV_AT.index(j)
                            if w == 0:
                                if B1:
                                    products(b - 2, 5, k, kt)
                            elif w == 2:
                                if B1:
                                    products(b - 2, 7, k, kt)
                            elif bb is not None:
                                products(bb, wb - 1, kb, kt)
                        if A:
                            score_tile(b, 2 * w + j // 2, 2 * j % 4 + 1, k)
                if A:
                    pe.wait_ge(s.maxed, (nB + b) * 64 + 64 + 2)
                    for t in range(TC):
                        last = nc.tensor.transpose(sc[0:H, 0, t * P:(t + 1) * P], top[:, t, :], S.ident[:, :])
                    last.then_inc(s.max_turned, 1)

            steps(pe, body)

        @block.scalar
        def _(act):
            def exps(bb, w):
                kp = w % 2
                act.wait_ge(s.pv_done, (nB + bb) * 8 + w + 1)
                for j in range(4):
                    act.wait_ge(s.st_done, (nB + bb) * 32 + 4 * w + j + 1)
                    nc.scalar.activation(prob[w % 2][:, j, 0:width(kp)], st[:, j % 2, 0:width(kp)], ACT.Exp,
                                         scale=a.scale).then_inc(s.exp_done, 1)

            def evacuate(bb, g):
                act.wait_ge(s.pv_done, (nB + bb) * 8 + 2 * g + 2 + 2)
                if not (isinstance(bb, int) and bb == 0 and call == 0 and g < 2):
                    act.wait_ge(s.pv_stored[g % 2], 32 * (nB + bb) + 16 * (g // 2))
                nc.scalar.activation(pv_sb[g % 2][:, :], pv[:, g % 2, :], ACT.Copy).then_inc(s.evacuated, 1)

            def body(b, A, B1, B2, k):
                for w, bb, wb, odd in waves(b, B1, B2):
                    if bb is not None:
                        exps(bb, wb)
                        if wb % 2 == 0 and wb > 0:
                            evacuate(bb, wb // 2 - 1)
                    if w == 2 and B1:
                        evacuate(b - 2, 3)

            steps(act, body)

        @block.vector
        def _(dve):
            for k in range(2):
                nc.vector.memset(kk[k][64:ROWS + 3, :, :], 1.0).then_inc(s.ready, 1)

            def body(b, A, B1, B2, k):
                if not A:
                    return
                for n in range(H):
                    for t in range(TC):
                        w = (t + 1) * P if a.causal else L
                        dve.wait_ge(s.scored, (nB + b) * 64 + 4 * n + t + 1)
                        nc.vector.tensor_reduce(top[:, t, n:n + 1], sc[:, t % 2, 0:w], AX.X, ALU.max
                                                ).then_inc(s.maxed, 1)
                dve.wait_ge(s.max_turned, nB + b + 1)
                if not (isinstance(b, int) and b == 0 and call == 0):
                    dve.wait_ge(s.max_stored, 16 * (nB + b))
                chain = Chain(dve, s.max_step, 3 * (nB + b))
                chain(nc.vector.tensor_scalar(max_part[:, 0, :], sc[0:H, 0, :], -1.0, None, ALU.mult))
                chain(nc.vector.scalar_tensor_tensor(out=max_rest[:, :], in0=sc[0:H, 0, :], scalar=-1.0,
                                                     in1=max_part[:, 0, :], op0=ALU.mult, op1=ALU.subtract))
                chain(nc.vector.tensor_copy(max_part[:, 1, :], max_rest[:, :]))
                nc.vector.tensor_tensor(max_part[:, 2, :], max_rest[:, :], max_part[:, 1, :],
                                        ALU.subtract).then_inc(s.max_parts, 1)

            steps(dve, body)


def split3(chain, eng, src, rest, parts, between=lambda: None):
    chain(eng.tensor_copy(parts[:, 0, :], src))
    chain(eng.tensor_tensor(rest, src, parts[:, 0, :], ALU.subtract))
    between()
    chain(eng.tensor_copy(parts[:, 1, :], rest))
    return eng.tensor_tensor(parts[:, 2, :], rest, parts[:, 1, :], ALU.subtract)


def store_parts(sp, dst, c, parts, heads, of_q, sem):
    for i in range(3):
        for j in range(3):
            r = DH * (3 * i + j)
            sp.dma_start(dst[:, r:r + DH, chunk(c)], parts[:, i if of_q else j, :]).then_inc(sem, 16)


STORES = 16 * 19


def projection_semaphores(S):
    s, sem = State(), S.sem
    s.calls, s.q_steps = 0, 0
    s.h_copied = sem("pj_h")
    s.projected = sem("pj_projected")
    s.copied = sem("pj_copied")
    s.q_parts, s.k_parts = sem("pj_q_parts"), sem("pj_k_parts")
    s.q_step, s.k_step = sem("pj_q_step"), sem("pj_k_step")
    s.stored = [sem("pj_stored0"), sem("pj_stored1")]
    S.pj = s
    S.setup_primes += [(s.copied, 3), (s.q_parts, 2), (s.k_parts, 2), (s.stored[0], STORES), (s.stored[1], STORES)]


def layer0_project(nc, S, inp, a):
    s, sem = S.pj, S.sem
    s.calls += 1
    s.q_steps += 8 * NB
    minned, expd, sigma, retrieved, merged = (sem(f"m0_{n}") for n in ("min", "exp", "sigma", "num_den", "merged"))
    loaded, prepared, ready = sem("m0_loaded"), sem("m0_prepared"), sem("m0_ready")
    KV = a.KVH * DH
    with ExitStack() as ctx:
        def sb(name, shape, dt=F32):
            return ctx.enter_context(nc.sbuf_tensor(f"p0_{name}", shape, dt))

        def ps(name, shape):
            return ctx.enter_context(nc.psum_tensor(f"p0_{name}", shape, F32))

        wq, wkv = sb("wq", [D, D]), sb("wkv", [D, 2 * KV])
        mem, norm, norm_w = sb("mem", [P, P]), sb("norm", [P, 1]), sb("norm_w", [P, P])
        hc = [sb(f"h{k}", [P, L]) for k in range(2)]
        qf, kf = [sb(f"q{k}", [P, L]) for k in range(2)], [sb(f"k{k}", [KV, L]) for k in range(2)]
        vf = [sb(f"v{k}", [P, TC, KV]) for k in range(2)]
        qp, kp = [sb(f"qp{k}", [P, 3, L], BF16) for k in range(2)], [sb(f"kp{k}", [KV, 3, L], BF16) for k in range(2)]
        q_rest, k_rest = sb("q_rest", [P, L]), sb("k_rest", [KV, L])
        low, high, e, sg = sb("low", [P, L]), sb("high", [P, L]), sb("e", [P, L]), sb("sg", [P, L])
        inv = sb("inv", [P, L])
        q_ps, k_ps, v_ps = ps("q_ps", [P, L]), ps("k_ps", [P, L]), ps("v_ps", [P, TC, P])
        num, den = ps("num", [P, L]), ps("den", [P, L])
        block = ctx.enter_context(nc.Block())

        @block.sync
        def _(sp):
            sp.dma_start(wq[:, :], inp["L0_attn_Wq"]).then_inc(loaded, 16)
            sp.dma_start(wkv[:, 0:KV], inp["L0_attn_Wk"]).then_inc(loaded, 16)
            sp.dma_start(wkv[:, KV:], inp["L0_attn_Wv"]).then_inc(loaded, 16)
            sp.dma_start(S.w_mem[:, :], across(inp["L0_attn_memory_weight"], 1)).then_inc(loaded, 16)
            sp.wait_ge(ready, 1)
            for g in range(2):
                sp.dma_start(mem[KV * g:KV * g + KV, KV * g:KV * g + KV], inp["L0_attn_memory"]).then_inc(loaded, 16)
                sp.dma_start(norm[KV * g:KV * g + KV, :],
                             inp["L0_attn_memory_norm"].rearrange("(p o) -> p o", o=1)).then_inc(loaded, 16)
            with sp.Fori(0, NB // 2) as i:
                for k in range(2):
                    c = 2 * i + k
                    sp.wait_ge(s.copied, 3 * c + 6)
                    alone(sp, S)
                    sp.dma_start(a.v[chunk(c), :].rearrange("(t p) n -> p t n", p=P), vf[k][:, :, :]
                                 ).then_inc(s.stored[k], 16)
                    sp.wait_ge(s.q_parts, c + 3)
                    alone(sp, S)
                    store_parts(sp, a.q_rows, c, qp[k], H, True, s.stored[k])
                    sp.wait_ge(s.k_parts, c + 3)
                    alone(sp, S)
                    store_parts(sp, a.k_rows, c, kp[k], a.KVH, False, s.stored[k])
            for k in range(2):
                sp.wait_ge(s.stored[k], STORES * (NB // 2 + 1))

        @block.tensor
        def _(pe):
            pe.wait_ge(loaded, 16 * 8)
            pe.wait_ge(prepared, 2)

            def project(c, k):
                pe.wait_ge(s.copied, 3 * c + 1)
                nc.tensor.matmul(q_ps[:, :], wq[:, :], S.h[:, chunk(c)], start=True, stop=True
                                 ).then_inc(s.projected, 1)
                pe.wait_ge(s.copied, 3 * c + 2)
                nc.tensor.matmul(k_ps[:, :], wkv[:, :], S.h[:, chunk(c)], start=True, stop=True
                                 ).then_inc(s.projected, 1)
                pe.wait_ge(s.copied, 3 * c + 3)
                pe.wait_ge(s.h_copied, c + 1)
                for t in range(TC):
                    last = nc.tensor.matmul(v_ps[:, t, 0:KV], hc[k][:, t * P:(t + 1) * P], wkv[:, KV:],
                                            start=True, stop=True)
                last.then_inc(s.projected, 1)

            def retrieve(c):
                pe.wait_ge(sigma, c + 1)
                pe.wait_ge(merged, c + 1)
                nc.tensor.matmul(num[:, :], mem[:, :], sg[:, :], start=True, stop=True)
                nc.tensor.matmul(den[:, :], norm_w[:, :], sg[:, :], start=True, stop=True).then_inc(retrieved, 1)

            project(0, 0)
            project(1, 1)
            retrieve(0)
            with pe.Fori(0, NB // 2 - 1) as i:
                for k in range(2):
                    project(2 * i + 2 + k, k)
                    retrieve(2 * i + 1 + k)
            retrieve(NB - 1)

        @block.scalar
        def _(act):
            act.wait_ge(loaded, 16 * 8)
            nc.scalar.activation(S.w_mem[:, :], S.w_mem[:, :], ACT.Sigmoid).then_inc(prepared, 1)
            with act.Fori(0, NB // 2) as i:
                for k in range(2):
                    c = 2 * i + k
                    act.wait_ge(s.projected, 3 * c + 1)
                    act.wait_ge(s.q_parts, c + 1)
                    nc.scalar.activation(qf[k][:, :], q_ps[:, :], ACT.Copy).then_inc(s.copied, 1)
                    act.wait_ge(s.projected, 3 * c + 2)
                    act.wait_ge(s.k_parts, c + 1)
                    nc.scalar.activation(kf[k][:, :], k_ps[0:KV, :], ACT.Copy).then_inc(s.copied, 1)
                    act.wait_ge(s.projected, 3 * c + 3)
                    act.wait_ge(s.stored[k], STORES // 2 * (c - k) + STORES)
                    nc.scalar.activation(vf[k][:, :, :], v_ps[:, :, 0:KV], ACT.Copy).then_inc(s.copied, 1)
                    act.wait_ge(minned, c + 1)
                    nc.scalar.activation(e[:, :], low[:, :], ACT.Tanh, scale=0.5).then_inc(expd, 1)

        @block.gpsimd
        def _(pool):
            with pool.Fori(0, NB // 2) as i:
                for k in range(2):
                    c = 2 * i + k
                    pool.wait_ge(s.projected, 3 * c + 1)
                    alone(pool, S)
                    nc.gpsimd.tensor_copy(hc[k][:, :], S.h[:, chunk(c)]).then_inc(s.h_copied, 1)
                    pool.wait_ge(s.copied, 3 * c + 5)
                    pool.wait_ge(s.stored[k], STORES // 2 * (c - k) + STORES)
                    alone(pool, S)
                    chain = Chain(pool, s.k_step, 3 * c)
                    split3(chain, nc.gpsimd, kf[k][:, :], k_rest[:, :], kp[k],
                           lambda: alone(pool, S)).then_inc(s.k_parts, 1)

        @block.vector
        def _(dve):
            dve.sem_inc(merged, 1)
            nc.vector.memset(mem[:, :], 0.0).then_inc(ready, 1)
            nc.vector.memset(norm_w[:, :], 0.0).then_inc(ready, 1)
            dve.wait_ge(ready, 2)
            for g in range(2):
                nc.vector.memset(norm_w[KV * g:KV * g + KV, KV * g:KV * g + KV], 1.0).then_inc(ready, 1)
            dve.wait_ge(prepared, 1)
            dve.wait_ge(ready, 4)
            nc.vector.tensor_scalar(S.w_dot[:, :], S.w_mem[:, :], -1.0, 1.0, ALU.mult, ALU.add)
            nc.vector.tensor_scalar(norm_w[:, :], norm_w[:, :], norm[:, 0:1], None, ALU.mult).then_inc(prepared, 1)

            def split_q(c, k, base):
                dve.wait_ge(s.copied, 3 * c + 4)
                nc.vector.tensor_scalar(low[:, :], qf[k][:, :], 0.0, None, ALU.min).then_inc(minned, 1)
                if not (isinstance(c, int) and c == 0):
                    dve.wait_ge(sigma, c)
                nc.vector.tensor_scalar(high[:, :], qf[k][:, :], 0.0, None, ALU.max)
                dve.wait_ge(s.stored[k], STORES // 2 * (c - k) + STORES)
                split3(Chain(dve, s.q_step, base), nc.vector, qf[k][:, :], q_rest[:, :], qp[k]).then_inc(s.q_parts, 1)

            def elu(c, base):
                chain = Chain(dve, s.q_step, base)
                dve.wait_ge(expd, c + 1)
                chain(nc.vector.tensor_scalar(sg[:, :], e[:, :], -1.0, 1.0, ALU.mult, ALU.add))
                chain(nc.vector.reciprocal(sg[:, :], sg[:, :]))
                chain(nc.vector.tensor_tensor(sg[:, :], e[:, :], sg[:, :], ALU.mult))
                nc.vector.scalar_tensor_tensor(out=sg[:, :], in0=sg[:, :], scalar=2.0, in1=high[:, :],
                                               op0=ALU.mult, op1=ALU.add).then_inc(sigma, 1)

            def merge(c, base):
                chain = Chain(dve, s.q_step, base)
                dve.wait_ge(retrieved, c + 1)
                chain(nc.vector.reciprocal(inv[:, :], den[:, :]))
                chain(nc.vector.tensor_tensor(inv[:, :], num[:, :], inv[:, :], ALU.mult))
                nc.vector.scalar_tensor_tensor(out=S.x[:, chunk(c)], in0=inv[:, :], scalar=S.w_mem[:, 0:1],
                                               in1=S.x[:, chunk(c)], op0=ALU.mult, op1=ALU.add).then_inc(merged, 1)

            def chunk_after(c, k):
                split_q(c, k, 8 * c - 2)
                merge(c - 1, 8 * c + 1)
                elu(c, 8 * c + 3)

            split_q(0, 0, 0)
            elu(0, 3)
            chunk_after(1, 1)
            with dve.Fori(0, NB // 2 - 1) as i:
                for k in range(2):
                    chunk_after(2 * i + 2 + k, k)
            merge(NB - 1, 8 * NB - 2)


def combine(nc, S, a, dst, weight=None):
    sem, nm = S.sem, a.name
    den_loaded, inverse, picked = sem(f"{nm}_den_loaded"), sem(f"{nm}_inverse"), sem(f"{nm}_picked")
    num_loaded = [sem(f"{nm}_num_loaded{k}") for k in range(4)]
    spread, multiplied = sem(f"{nm}_spread"), sem(f"{nm}_multiplied")
    with ExitStack() as ctx:
        num = ctx.enter_context(nc.sbuf_tensor(f"{nm}_num", [P, 4, L], F32))
        den = ctx.enter_context(nc.sbuf_tensor(f"{nm}_den", [P, L], F32))
        pick = ctx.enter_context(nc.sbuf_tensor(f"{nm}_pick", [P, NB, P], F32))
        inv = ctx.enter_context(nc.psum_tensor(f"{nm}_inv", [P, 4, L], F32))
        rows = a.pv.rearrange("b g (j r) n -> (b g j) r n", j=4)
        block = ctx.enter_context(nc.Block())

        @block.sync
        def _(sp):
            sp.dma_start(den[:, :], rows[:, DH, :]).then_inc(den_loaded, 16)
            for b in range(NB):
                if b >= 4:
                    sp.wait_ge(multiplied, b - 3)
                sp.dma_start(num[:, b % 4, :], rows[H * b:H * b + H, 0:DH, :]).then_inc(num_loaded[b % 4], 16)

        @block.gpsimd
        def _(pool):
            nc.gpsimd.memset(pick[:, :, :], 0.0).then_inc(picked, 1)
            pool.wait_ge(picked, 1)
            view = pick[:, :, :].rearrange("k b (h d) -> k (b h) d", d=DH)
            nc.gpsimd.affine_select(out=view, in_=view, compare_op=ALU.not_equal, fill=1.0, base=0,
                                    pattern=[[-1, P], [0, DH]], channel_multiplier=1).then_inc(picked, 1)

        @block.tensor
        def _(pe):
            pe.wait_ge(picked, 2)
            pe.wait_ge(inverse, 1)
            for b in range(NB):
                if b >= 4:
                    pe.wait_ge(multiplied, b - 3)
                nc.tensor.matmul(inv[:, b % 4, :], pick[:, b, :], den[:, :], start=True, stop=True).then_inc(spread, 1)

        @block.vector
        def _(dve):
            dve.wait_ge(den_loaded, 16)
            nc.vector.reciprocal(den[:, :], den[:, :]).then_inc(inverse, 1)
            for b in range(NB):
                dve.wait_ge(num_loaded[b % 4], 16 * (b // 4 + 1))
                dve.wait_ge(spread, b + 1)
                to = dst[:, b * L:(b + 1) * L]
                if weight is None:
                    nc.vector.tensor_tensor(to, num[:, b % 4, :], inv[:, b % 4, :], ALU.mult).then_inc(multiplied, 1)
                else:
                    nc.vector.tensor_tensor(num[:, b % 4, :], num[:, b % 4, :], inv[:, b % 4, :], ALU.mult
                                            ).then_inc(inverse, 1)
                    dve.wait_ge(inverse, b + 2)
                    nc.vector.scalar_tensor_tensor(out=to, in0=num[:, b % 4, :], scalar=weight, in1=to,
                                                   op0=ALU.mult, op1=ALU.add).then_inc(multiplied, 1)


def layer0_attention(nc, S, inp):
    a = new_attention(nc, S, "a0", 8, False)
    layer0_project(nc, S, inp, a)
    attend(nc, S, a)
    combine(nc, S, a, S.x, S.w_dot[:, 0:1])


def pattention_semaphores(S):
    s, sem = State(), S.sem
    s.calls = s.step_base = 0
    s.h_copied = sem("pt_h")
    s.scored = sem("pt_scored")
    s.negated = sem("pt_negated")
    s.expd = sem("pt_expd")
    s.normed = sem("pt_normed")
    s.turned = sem("pt_turned")
    s.taken = sem("pt_taken")
    s.summed = sem("pt_summed")
    s.merged = sem("pt_merged")
    s.step = sem("pt_step")
    S.pt = s
    S.setup_primes += [(s.expd, 2), (s.turned, 4), (s.taken, 2), (s.summed, 2), (s.merged, 1)]


def pattention(nc, S, name, src, keys, values, groups, a=None, merge=None):
    s, pj = S.pt, S.pj
    call = s.calls
    s.calls += 1
    nt = sum(groups)
    ng = len(groups)
    first = [sum(groups[:g]) for g in range(ng)]
    scale = float(D) ** -0.5
    c0, t0 = NB * call, NT * call
    if a is not None:
        pc, s0 = NB * pj.calls, 4 * STORES * pj.calls
        pj.calls += 1
    with ExitStack() as ctx:
        def sb(n, shape, dt=F32):
            return ctx.enter_context(nc.sbuf_tensor(f"{name}_{n}", shape, dt))

        def ps(n, shape):
            return ctx.enter_context(nc.psum_tensor(f"{name}_{n}", shape, F32))

        hc = [sb(f"h{k}", [P, L]) for k in range(2)]
        prob = sb("prob", [P, 4, nt, P])
        turned = [sb(f"turned{k}", [P, nt, L]) for k in range(2)]
        top, neg, total, inv = (sb(n, [P, 4, ng]) for n in ("top", "neg", "total", "inv"))
        sc, tp = ps("sc", [P, 2, L]), ps("tp", [P, 2, L])
        if a is not None:
            qf, kf, vf = ([sb(f"{n}f{k}", [P, L]) for k in range(2)] for n in "qkv")
            qp, kp = ([sb(f"{n}p{k}", [P, 3, L], BF16) for k in range(2)] for n in "qk")
            q_rest, k_rest = sb("q_rest", [P, L]), sb("k_rest", [P, L])
            outs = [ps(f"{n}_ps", [P, L]) for n in "qkv"]
        else:
            y = ps("y", [P, L])
        block = ctx.enter_context(nc.Block())

        def tile(i, u):
            return t0 + 8 * i + u

        if a is not None:
            @block.sync
            def _(sp):
                with sp.Fori(0, NB // 2) as i:
                    for k in range(2):
                        c = 2 * i + k
                        sp.wait_ge(pj.copied, 3 * (pc + c) + 6)
                        alone(sp, S)
                        sp.dma_start(a.v[chunk(c), :].rearrange("(t p) n -> p t n", p=P),
                                     vf[k][:, :].rearrange("p (t n) -> p t n", t=TC)).then_inc(pj.stored[k], 16)
                        sp.wait_ge(pj.q_parts, pc + c + 3)
                        alone(sp, S)
                        store_parts(sp, a.q_rows, c, qp[k], H, True, pj.stored[k])
                        sp.wait_ge(pj.k_parts, pc + c + 3)
                        alone(sp, S)
                        store_parts(sp, a.k_rows, c, kp[k], a.KVH, False, pj.stored[k])
                for k in range(2):
                    sp.wait_ge(pj.stored[k], s0 + STORES * (NB // 2 + 1))

        @block.gpsimd
        def _(pool):
            def copy_h(c, k):
                pool.wait_ge(s.summed, c0 + c + 1)
                alone(pool, S)
                nc.gpsimd.tensor_copy(hc[k][:, :], src[:, chunk(c)]).then_inc(s.h_copied, 1)

            def split_k(c, i, k):
                pool.wait_ge(pj.copied, 3 * (pc + c) + 5)
                pool.wait_ge(pj.stored[k], s0 + STORES * i + STORES)
                alone(pool, S)
                chain = Chain(pool, pj.k_step, 3 * (pc + c))
                split3(chain, nc.gpsimd, kf[k][:, :], k_rest[:, :], kp[k],
                       lambda: alone(pool, S)).then_inc(pj.k_parts, 1)

            for k in range(2):
                copy_h(k, k)
            with pool.Fori(0, NB // 2 - 1) as i:
                for k in range(2):
                    copy_h(2 * i + 2 + k, k)
                    if a is not None:
                        split_k(2 * i + k, i, k)
            if a is not None:
                for k in range(2):
                    split_k(NB - 2 + k, NB // 2 - 1, k)

        @block.tensor
        def _(pe):
            if s.loaded_count:
                pe.wait_ge(s.loaded, s.loaded_count)
            with pe.Fori(0, NB // 2) as i:
                for u in range(10):
                    if u < 8:
                        k, t = u // 4, u % 4
                        if t == 0:
                            pe.wait_ge(s.h_copied, c0 + 2 * i + k + 1)
                        pe.wait_ge(s.expd, tile(i, u) + 1)
                        nc.tensor.matmul(sc[:, u % 2, 0:nt * P], hc[k][:, t * P:(t + 1) * P], keys, start=True,
                                         stop=True).then_inc(s.scored, 1)
                    if u >= 2:
                        v = u - 2
                        pe.wait_ge(s.normed, tile(i, v) + 1)
                        pe.wait_ge(s.taken, tile(i, v) + 1)
                        for n in range(nt):
                            last = nc.tensor.transpose(tp[:, v % 2, n * P:(n + 1) * P], prob[:, v % 4, n, :],
                                                       S.ident[:, :])
                        last.then_inc(s.turned, 1)
                        if v % 4 == 3:
                            k = v // 4
                            c = 2 * i + k
                            pe.wait_ge(s.taken, tile(i, v) + 3)
                            if a is not None:
                                for n in range(2):
                                    pe.wait_ge(pj.copied, 3 * (pc + c) + n + 1)
                                    nc.tensor.matmul(outs[n][:, :], values[n], turned[k][:, n, :], start=True,
                                                     stop=True).then_inc(pj.projected, 1)
                                pe.wait_ge(pj.copied, 3 * (pc + c) + 3)
                                for t in range(TC):
                                    last = nc.tensor.matmul(outs[2][:, t * P:(t + 1) * P],
                                                            turned[k][:, 2, t * P:(t + 1) * P], values[2],
                                                            start=True, stop=True)
                                last.then_inc(pj.projected, 1)
                                pe.sem_inc(s.summed, 1)
                            else:
                                pe.wait_ge(s.merged, s.merged_base + c + 1)
                                for n in range(nt):
                                    last = nc.tensor.matmul(y[:, :], values[n], turned[k][:, n, :], start=(n == 0),
                                                            stop=(n == nt - 1))
                                last.then_inc(s.summed, 1)

        @block.scalar
        def _(act):
            with act.Fori(0, NB // 2) as i:
                for u in range(10):
                    if u < 8:
                        act.wait_ge(s.negated, tile(i, u) + 1)
                        act.wait_ge(s.turned, tile(i, u) + 1)
                        for g in range(ng):
                            last = nc.scalar.activation(
                                prob[:, u % 4, first[g]:first[g] + groups[g], :],
                                sc[:, u % 2, first[g] * P:(first[g] + groups[g]) * P].rearrange("p (n m) -> p n m", m=P),
                                ACT.Exp, bias=neg[:, u % 4, g:g + 1], scale=scale,
                                accum_out=total[:, u % 4, g:g + 1])
                        last.then_inc(s.expd, 1)
                    if u >= 2:
                        v = u - 2
                        k = v // 4
                        act.wait_ge(s.turned, tile(i, v) + 5)
                        if v % 4 == 0:
                            act.wait_ge(s.summed, c0 + 2 * i + k + 1)
                        nc.scalar.activation(turned[k][:, :, (v % 4) * P:(v % 4 + 1) * P],
                                             tp[:, v % 2, 0:nt * P].rearrange("p (n m) -> p n m", m=P),
                                             ACT.Copy).then_inc(s.taken, 1)
                        if v % 4 == 3 and a is not None:
                            c = 2 * i + k
                            act.wait_ge(pj.projected, 3 * (pc + c) + 1)
                            act.wait_ge(pj.q_parts, pc + c + 1)
                            nc.scalar.activation(qf[k][:, :], outs[0][:, :], ACT.Copy).then_inc(pj.copied, 1)
                            act.wait_ge(pj.projected, 3 * (pc + c) + 2)
                            act.wait_ge(pj.k_parts, pc + c + 1)
                            nc.scalar.activation(kf[k][:, :], outs[1][:, :], ACT.Copy).then_inc(pj.copied, 1)
                            act.wait_ge(pj.projected, 3 * (pc + c) + 3)
                            act.wait_ge(pj.stored[k], s0 + STORES * i + STORES)
                            nc.scalar.activation(vf[k][:, :], outs[2][:, :], ACT.Copy).then_inc(pj.copied, 1)

        @block.vector
        def _(dve):
            def negate(i, u):
                dve.wait_ge(s.scored, tile(i, u) + 1)
                chain = Chain(dve, s.step, s.step_base + 16 * i + max(2 * u - 1, 0))
                chain(nc.vector.tensor_reduce(top[:, u % 4, :],
                                              sc[:, u % 2, 0:nt * P].rearrange("p (g m) -> p g m", g=ng), AX.X, ALU.max))
                nc.vector.tensor_scalar(neg[:, u % 4, :], top[:, u % 4, :], -scale, None, ALU.mult
                                        ).then_inc(s.negated, 1)

            def norm(i, u):
                dve.wait_ge(s.expd, tile(i, u) + 3)
                chain = Chain(dve, s.step, s.step_base + 16 * i + 2 * u + (2 if u < 7 else 1))
                chain(nc.vector.reciprocal(inv[:, u % 4, :], total[:, u % 4, :]))
                for g in range(ng):
                    p = prob[:, u % 4, first[g]:first[g] + groups[g], :]
                    last = nc.vector.tensor_scalar(p, p, inv[:, u % 4, g:g + 1], None, ALU.mult)
                last.then_inc(s.normed, 1)

            with dve.Fori(0, NB // 2) as i:
                negate(i, 0)
                for u in range(8):
                    if u < 7:
                        negate(i, u + 1)
                    norm(i, u)
                    if a is None and u == 7:
                        for k in range(2):
                            dve.wait_ge(s.summed, c0 + 2 * i + k + 3)
                            merge(dve, 2 * i + k, y)
                    if a is not None and u >= 6:
                        k = u - 6
                        c = 2 * i + k
                        dve.wait_ge(pj.copied, 3 * (pc + c) + 4)
                        dve.wait_ge(pj.stored[k], s0 + STORES * i + STORES)
                        chain = Chain(dve, pj.q_step, pj.q_steps + 3 * c)
                        split3(chain, nc.vector, qf[k][:, :], q_rest[:, :], qp[k]).then_inc(pj.q_parts, 1)
        s.step_base += 16 * NB // 2


def layer1_attention(nc, S, inp):
    a = new_attention(nc, S, "a1", 16, True)
    s = S.pt
    with ExitStack() as ctx:
        def sb(n, shape, dt=F32):
            return ctx.enter_context(nc.sbuf_tensor(f"a1_{n}", shape, dt))

        g = sb("g", [D, T])
        keys, fkeys, pkeys = sb("keys", [D, 3 * P]), sb("fkeys", [D, 4 * P]), sb("pkeys", [D, P])
        values, fvalues, pvalues = sb("values", [P, 3, D]), sb("fvalues", [P, 4, D]), sb("pvalues", [P, D])
        s.loaded = S.sem("a1_loaded")
        loads = [(keys[:, 0:P], inp["a1_qKT"]), (keys[:, P:2 * P], inp["a1_kKT"]), (keys[:, 2 * P:], inp["a1_vKT"]),
                 (values[:, 0, :], inp["L1_attn_qV"]), (values[:, 1, :], inp["L1_attn_kV"]),
                 (values[:, 2, :], inp["L1_attn_vV"]), (pkeys[:, :], inp["a1_pKT"]), (pvalues[:, :], inp["L1_attn_pV"]),
                 (fkeys[:, :], inp["a1_fKT"]), (fvalues[:, :, :], inp["L1_attn_fV"].rearrange("(n p) c -> p n c", p=P))]
        S.pending += [(dst, src, s.loaded) for dst, src in loads]
        s.loaded_count = 16 * len(loads)
        layer_norm(nc, S, S.h, g)
        pattention(nc, S, "a1q", g, keys[:, :], [values[:, n, :] for n in range(3)], [1, 1, 1], a=a)
        attend(nc, S, a)
        combine(nc, S, a, g)

        def merge_inner(dve, c, y):
            nc.vector.tensor_tensor(g[:, chunk(c)], S.h[:, chunk(c)], y[:, :], ALU.add).then_inc(s.merged, 1)

        s.merged_base = 0
        pattention(nc, S, "a1p", g, pkeys[:, :], [pvalues[:, :]], [1], merge=merge_inner)
        layer_norm(nc, S, g, S.h)

        def merge_outer(dve, c, y):
            nc.vector.tensor_tensor(g[:, chunk(c)], g[:, chunk(c)], y[:, :], ALU.add).then_inc(s.merged, 1)
            dve.wait_ge(s.merged, s.merged_base + c + 2)
            nc.vector.tensor_tensor(S.x[:, chunk(c)], S.x[:, chunk(c)], g[:, chunk(c)], ALU.add)

        s.merged_base = NB
        pattention(nc, S, "a1f", S.h, fkeys[:, :], [fvalues[:, n, :] for n in range(4)], [4], merge=merge_outer)


LOG1P = ((1.0091787943684127, 1.1116931889027009), (-0.08503787137606685, 3.273833261641785),
         (-1.43055840539456, 2.7158022586526567), (-2.329466773006516, 0.4346164918572432))
LOG1P_SCALE = 0.0051261021233726485


def layer2_mamba(nc, S, inp):
    sem = S.sem
    INNER, STATES, RANK, TAPS = 2 * D, 16, D // 16, 4
    H2 = INNER // P
    UNITS = 2 * NB
    LAG = 3
    PAIRED = (1, 4, 6, 11)
    with ExitStack() as ctx:
        def sb(n, shape, dt=F32):
            return ctx.enter_context(nc.sbuf_tensor(f"a2_{n}", shape, dt))

        out = sb("out", [P, T])
        proj, small = sb("proj", [P, H2, D]), sb("small", [P, 3])
        loaded, prepared, stepped, limited = (sem(f"a2_{n}") for n in ("loaded", "prepared", "stepped", "limited"))
        with ExitStack() as inner:
            def si(n, shape, dt=F32):
                return inner.enter_context(nc.sbuf_tensor(f"a2_{n}", shape, dt))

            cols = {}
            width = 0
            for name, n in (("in", 2 * INNER), ("xproj", H2 * (96 + RANK)), ("out", H2 * D), ("dt_b", H2),
                            ("conv_b", H2), ("Dp", H2), ("Alog", H2 * STATES)):
                cols[name] = (width, width + n)
                width += n
            pack = [si(f"pack{d}", [P, width]) for d in range(2)]

            def w(d, name):
                lo, hi = cols[name]
                return pack[d][:, lo:hi]

            taps = [si(f"taps{d}", [P, TAPS, INNER]) for d in range(2)]
            dt_w = [si(f"dt_w{d}", [96 + RANK, INNER]) for d in range(2)]
            diag = [si(f"diag{d}", [P, H2, P]) for d in range(2)]
            neg_a = [si(f"neg_a{d}", [P, H2 * STATES]) for d in range(2)]
            capped_a = [si(f"capped_a{d}", [P, H2, STATES]) for d in range(2)]
            peak = si("peak", [P, H2, 1])
            m1, m2 = si("m1", [96, 1]), si("m2", [96, 1])
            u, sz, delta, du = (si(n, [P, 2, H2, L]) for n in ("u", "sz", "delta", "du"))
            soft_t, soft_r = (si(n, [P, H2, L]) for n in ("soft_t", "soft_r"))
            square = si("square", [P, 2, H2, L])
            shifts = si("shifts", [P, len(LOG1P)])
            xp = si("xp", [96 + RANK, L])
            part0, part1 = si("part0", [96, L], BF16), si("part1", [96, L], BF16)
            bc = [si(f"bc{d}", [96, L], BF16) for d in range(2)]
            drive = si("drive", [P, 2, H2, L])
            decay = si("decay", [P, 4, H2, L])
            c_copy = si("c_copy", [P, 4, L])
            g = si("g", [P, 8, H2, L])
            gated, o = si("gated", [P, H2, L]), si("o", [P, 2, L])
            bank = inner.enter_context(nc.psum_tensor("a2_bank", [P, 2, L], F32))
            y = inner.enter_context(nc.psum_tensor("a2_y", [P, H2, L], F32))
            b_all = inner.enter_context(nc.psum_tensor("a2_b", [P, 2, L], F32))
            c_all = inner.enter_context(nc.psum_tensor("a2_c", [P, 2, L], F32))

            with nc.Block() as block:
                @block.sync
                def _(sp):
                    for d, (pk, cv, dw) in enumerate(((inp["a2_fw_packT"], inp["a2_fw_convT"], inp["a2_fw_dtT"]),
                                                      (inp["a2_bw_packT"], inp["a2_bw_convT"], inp["a2_bw_dtT"]))):
                        sp.dma_start(pack[d][:, :], pk).then_inc(loaded, 16)
                        sp.dma_start(taps[d][:, :, :].rearrange("p j c -> p (j c)"), across(cv, TAPS * INNER)
                                     ).then_inc(loaded, 16)
                        sp.dma_start(dt_w[d][96:, :], dw).then_inc(loaded, 16)
                    sp.dma_start(proj[:, :, :].rearrange("p k c -> p (k c)"), inp["a2_projT"]).then_inc(loaded, 16)
                    sp.dma_start(small[:, :], inp["a2_smallT"]).then_inc(loaded, 16)

                @block.vector
                def _(dve):
                    for q, (shift, _) in enumerate(LOG1P):
                        nc.vector.memset(shifts[:, q:q + 1], shift)
                    nc.vector.memset(m1[0:32, :], 0.0)
                    nc.vector.memset(m1[32:64, :], -1.0)
                    nc.vector.memset(m1[64:96, :], -1.0)
                    nc.vector.memset(m2[0:32, :], 0.0)
                    nc.vector.memset(m2[32:64, :], 0.0)
                    nc.vector.memset(m2[64:96, :], -1.0)
                    dve.wait_ge(loaded, 8 * 16)
                    for d in range(2):
                        nc.vector.tensor_scalar(w(d, "Alog"), w(d, "Alog"), 88.0, None, ALU.min).then_inc(limited, 1)
                    for d in range(2):
                        nc.vector.tensor_tensor(
                            taps[d][:, :, :], taps[d][:, :, :],
                            w(d, "in")[:, 0:INNER].rearrange("p (o c) -> p o c", o=1).to_broadcast([P, TAPS, INNER]),
                            ALU.mult)
                        for k in range(H2):
                            nc.vector.tensor_scalar(diag[d][:, k, :], S.ident[:, :], w(d, "Dp")[:, k:k + 1], None,
                                                    ALU.mult)
                        dve.wait_ge(prepared, d + 1)
                        nc.vector.tensor_scalar(neg_a[d][:, :], neg_a[d][:, :], -1.0, None, ALU.mult)

                @block.scalar
                def _(act):
                    act.wait_ge(limited, 2)
                    for d in range(2):
                        nc.scalar.activation(neg_a[d][:, :], w(d, "Alog"), ACT.Exp).then_inc(prepared, 1)

            conv_done, u_done, z_done, sz_done = (sem(f"a2_{n}_done") for n in ("conv", "u", "z", "sz"))
            xproj_done, xp_copied, parts_done = sem("a2_xproj_done"), sem("a2_xp_copied"), sem("a2_parts_done")
            dpre_done, soft_read, soft_done = sem("a2_dpre_done"), sem("a2_soft_read"), sem("a2_soft_done")
            squared, multiplied, paired = sem("a2_squared"), sem("a2_multiplied"), sem("a2_paired")
            delta_done, du_done, dve_step = sem("a2_delta_done"), sem("a2_du_done"), sem("a2_dve_step")
            b_done, c_done, c_copied, decay_done = (sem(f"a2_{n}") for n in ("b_done", "c_done", "c_copied", "decay_done"))
            drive_done, scanned, g_done, g_used = (sem(f"a2_{n}") for n in ("drive_done", "scanned", "g_done", "g_used"))
            y_done, gated_done, o_summed, o_done, p_summed, p_done = (
                sem(f"a2_{n}") for n in ("y_done", "gated_done", "o_summed", "o_done", "p_summed", "p_done"))
            STEPS_DVE = 8

            def wait(eng, s, value):
                if not isinstance(value, int) or value > 0:
                    eng.wait_ge(s, value)

            def h_of(b, off=0, n=L):
                return S.h[:, bass.ds(b * L + off, n)]

            def out_of(b):
                return out[:, bass.ds(b * L, L)]

            def pe_gate_sum(U, d, n):
                if n in PAIRED:
                    return
                if n - 1 in PAIRED:
                    nc.tensor.wait_ge(paired, len(PAIRED) * U + PAIRED.index(n - 1) + 1)
                nc.tensor.wait_ge(g_done, STATES * U + n + 1)
                if n == 0:
                    wait(nc.tensor, gated_done, U)
                for k in range(H2):
                    last = nc.tensor.matmul(y[:, k, :], S.ident[:, :], g[:, n % 8, k, :], start=(n == 0), stop=False)
                last.then_inc(g_used, 2 if n - 1 in PAIRED else 1)
                if n == STATES - 1:
                    for k in range(H2):
                        last = nc.tensor.matmul(y[:, k, :], diag[d][:, k, :], u[:, d, k, :], start=False, stop=True)
                    last.then_inc(y_done, 1)

            def pe_out(U, d):
                nc.tensor.wait_ge(gated_done, U + 1)
                for k in range(H2):
                    lo = cols["out"][0] + k * D
                    last = nc.tensor.matmul(bank[:, 0, :], pack[d][:, lo:lo + D], gated[:, k, :],
                                            start=(k == 0), stop=(k == H2 - 1))
                last.then_inc(o_summed, 1)

            def pe_project(b, U):
                nc.tensor.wait_ge(o_done, U + 1)
                for d in range(2):
                    last = nc.tensor.matmul(bank[:, 0, :], proj[:, d, :], o[:, d, :], start=(d == 0), stop=(d == 1))
                last.then_inc(p_summed, 1)

            def pe_conv(b, d, k, taps_now=tuple(reversed(range(TAPS)))):
                for j in taps_now:
                    shift = TAPS - 1 - j
                    n = L - shift
                    dst, src = (bank[:, k, shift:L], h_of(b, 0, n)) if d == 0 else (bank[:, k, 0:n], h_of(b, shift, n))
                    last = nc.tensor.matmul(dst, taps[d][:, j, k * P:(k + 1) * P], src,
                                            start=(j == TAPS - 1), stop=(j == 0))
                if taps_now[-1] == 0:
                    last.then_inc(conv_done, 1)

            def pe_z(b, d, V):
                for n, k in enumerate((1, 0)):
                    nc.tensor.wait_ge(u_done, 2 * V + n + 1)
                    nc.tensor.matmul(bank[:, k, :], pack[d][:, INNER + k * P:INNER + (k + 1) * P], h_of(b),
                                     start=True, stop=True).then_inc(z_done, 1)

            def pe_xproj(d, V):
                nc.tensor.wait_ge(sz_done, 2 * V + 1)
                for k in range(H2):
                    lo = cols["xproj"][0] + k * (96 + RANK)
                    last = nc.tensor.matmul(bank[0:96 + RANK, 1, :], pack[d][:, lo:lo + 96 + RANK], u[:, d, k, :],
                                            start=(k == 0), stop=(k == H2 - 1))
                last.then_inc(xproj_done, 1)

            def pe_dpre(d, V):
                nc.tensor.wait_ge(sz_done, 2 * V + 2)
                nc.tensor.wait_ge(xp_copied, V + 1)
                for k in range(H2):
                    nc.tensor.matmul(bank[:, k, :], dt_w[d][96:, k * P:(k + 1) * P], xp[96:, :],
                                     start=True, stop=True).then_inc(dpre_done, 1)

            def pe_spread(U, d, n):
                s = STATES * U + n
                if n == 0:
                    nc.tensor.wait_ge(parts_done, U + 1)
                wait(nc.tensor, drive_done, s - 1)
                nc.tensor.matmul(b_all[:, n % 2, :], S.sel[:, n, :], bc[d][:, :], start=True, stop=True
                                 ).then_inc(b_done, 1)
                wait(nc.tensor, c_copied, s - 1)
                nc.tensor.matmul(c_all[:, n % 2, :], S.sel[:, STATES + n, :], bc[d][:, :], start=True, stop=True
                                 ).then_inc(c_done, 1)

            def pe_unit(b, d, first, last_unit):
                U = 2 * b + d
                nb, nd = (b, 1) if d == 0 else (b + 1, 0)
                for n in range(STATES):
                    if n < STATES - 1:
                        pe_spread(U, d, n + 1)
                    elif not last_unit:
                        pe_spread(U + 1, nd, 0)
                    if n < TAPS and not last_unit:
                        if n == 0:
                            nc.tensor.wait_ge(soft_read, 2 * U + 2)
                        pe_conv(nb, nd, 1, (TAPS - 1 - n,))
                    if n >= LAG:
                        pe_gate_sum(U, d, n - LAG)
                    elif not first:
                        pe_gate_sum(U - 1, 1 - d, STATES - LAG + n)
                    if n == 4 and not first:
                        nc.tensor.wait_ge(soft_read, 2 * U + 1)
                        pe_out(U - 1, 1 - d)
                    if n == 5 and not first and d == 0:
                        pe_project(b - 1, U - 1)
                    if last_unit:
                        continue
                    if n == 6:
                        nc.tensor.wait_ge(soft_read, 2 * U + 1)
                        wait(nc.tensor, o_done, U)
                        wait(nc.tensor, p_done, b)
                        pe_conv(nb, nd, 0)
                    if n == 7:
                        pe_z(nb, nd, U + 1)
                    if n == 8:
                        pe_xproj(nd, U + 1)
                    if n == 9:
                        pe_dpre(nd, U + 1)

            def act_silu(d, V):
                for n, k in enumerate((1, 0)):
                    nc.scalar.wait_ge(conv_done, 2 * V + n + 1)
                    nc.scalar.activation(u[:, d, k, :], bank[:, k, :], ACT.Silu, bias=w(d, "conv_b")[:, k:k + 1]
                                         ).then_inc(u_done, 1)
                for n, k in enumerate((1, 0)):
                    nc.scalar.wait_ge(z_done, 2 * V + n + 1)
                    nc.scalar.activation(sz[:, d, k, :], bank[:, k, :], ACT.Silu).then_inc(sz_done, 1)

            def act_copy_xproj(V):
                nc.scalar.wait_ge(xproj_done, V + 1)
                wait(nc.scalar, parts_done, V)
                wait(nc.scalar, dpre_done, 2 * V)
                nc.scalar.activation(xp[:, :], bank[0:96 + RANK, 1, :], ACT.Copy).then_inc(xp_copied, 1)

            def act_soft(d, V):
                wait(nc.scalar, delta_done, V)
                for k in range(H2):
                    nc.scalar.wait_ge(dpre_done, 2 * V + k + 1)
                    nc.scalar.activation(soft_t[:, k, :], bank[:, k, :], ACT.Abs, bias=w(d, "dt_b")[:, k:k + 1])
                    nc.scalar.activation(soft_r[:, k, :], bank[:, k, :], ACT.Relu, bias=w(d, "dt_b")[:, k:k + 1]
                                         ).then_inc(soft_read, 1)
                nc.scalar.wait_ge(soft_read, 2 * V + 2)
                nc.scalar.activation(soft_t[:, :, :], soft_t[:, :, :], ACT.Exp, scale=-1.0).then_inc(soft_done, 1)
                nc.scalar.wait_ge(soft_done, V + 1)

            def act_square(V, q):
                wait(nc.scalar, multiplied, len(LOG1P) * V + q - 1)
                nc.scalar.activation(square[:, q % 2, :, :], soft_t[:, :, :], ACT.Square, bias=shifts[:, q:q + 1]
                                     ).then_inc(squared, 1)

            def act_decay(U, d, n):
                wait(nc.scalar, scanned, STATES * U + n - 3)
                for k in range(H2):
                    last = nc.scalar.activation(decay[:, n % 4, k, :], delta[:, d, k, :], ACT.Exp,
                                                scale=capped_a[d][:, k, n:n + 1])
                last.then_inc(decay_done, 1)

            def act_unit(b, d, first, last_unit):
                U = 2 * b + d
                nd = 1 - d
                nc.scalar.wait_ge(delta_done, U + 1)
                for n in range(STATES):
                    s = STATES * U + n
                    if n == 0:
                        act_decay(U, d, 0)
                    if n < STATES - 1:
                        act_decay(U, d, n + 1)
                    nc.scalar.wait_ge(c_done, s + 1)
                    wait(nc.scalar, g_done, s - 3)
                    nc.scalar.activation(c_copy[:, n % 4, :], c_all[:, n % 2, :], ACT.Copy).then_inc(c_copied, 1)
                    if n == 6 and not first and d == 0:
                        nc.scalar.wait_ge(p_summed, b)
                        nc.scalar.activation(out_of(b - 1), bank[:, 0, :], ACT.Identity, bias=small[:, 0:1]
                                             ).then_inc(p_done, 1)
                    if last_unit:
                        continue
                    if n == 7:
                        act_silu(nd, U + 1)
                    if n == 8:
                        act_copy_xproj(U + 1)
                    if n == 9:
                        act_soft(nd, U + 1)
                    if 10 <= n < 10 + len(LOG1P):
                        act_square(U + 1, n - 10)

            def dve_parts(d, V):
                chain = Chain(nc.vector, dve_step, STEPS_DVE * V)
                nc.vector.wait_ge(xp_copied, V + 1)
                chain(nc.vector.tensor_copy(part0[:, :], xp[0:96, :]))
                chain(nc.vector.scalar_tensor_tensor(xp[0:96, :], part0[:, :], m1[:, 0:1], xp[0:96, :], ALU.mult, ALU.add))
                chain(nc.vector.tensor_copy(part1[:, :], xp[0:96, :]))
                nc.vector.scalar_tensor_tensor(bc[d][:, :], part1[:, :], m2[:, 0:1], xp[0:96, :], ALU.mult, ALU.add
                                               ).then_inc(parts_done, 1)

            def dve_factor(d, V, q):
                nc.vector.wait_ge(squared, len(LOG1P) * V + q + 1)
                if q == 0:
                    nc.vector.wait_ge(soft_done, V + 1)
                else:
                    nc.vector.wait_ge(multiplied, len(LOG1P) * V + q)
                nc.vector.scalar_tensor_tensor(delta[:, d, :, :], square[:, q % 2, :, :], LOG1P[q][1],
                                               soft_t[:, :, :] if q == 0 else delta[:, d, :, :], ALU.add, ALU.mult
                                               ).then_inc(multiplied, 1)

            def dve_delta(d, V):
                chain = Chain(nc.vector, dve_step, STEPS_DVE * V + 3)
                nc.vector.wait_ge(multiplied, len(LOG1P) * (V + 1))
                chain(nc.vector.scalar_tensor_tensor(delta[:, d, :, :], delta[:, d, :, :], LOG1P_SCALE, soft_r[:, :, :],
                                                     ALU.mult, ALU.add))
                chain(nc.vector.tensor_reduce(peak[:, :, 0], delta[:, d, :, :], AX.X, ALU.max))
                chain(nc.vector.tensor_scalar(peak[:, :, :], peak[:, :, :], 1.0, None, ALU.max))
                chain(nc.vector.reciprocal(peak[:, :, :], peak[:, :, :]))
                chain(nc.vector.tensor_scalar(peak[:, :, :], peak[:, :, :], -2.0 ** 125, None, ALU.mult))
                nc.vector.tensor_tensor(capped_a[d][:, :, :], neg_a[d][:, :].rearrange("p (k n) -> p k n", k=H2),
                                        peak[:, :, :].to_broadcast([P, H2, STATES]), ALU.max).then_inc(delta_done, 1)
                nc.vector.wait_ge(delta_done, V + 1)
                nc.vector.tensor_tensor(du[:, d, :, :], delta[:, d, :, :], u[:, d, :, :], ALU.mult
                                        ).then_inc(du_done, 1)

            def dve_drive(U, d, n):
                s = STATES * U + n
                nc.vector.wait_ge(b_done, s + 1)
                wait(nc.vector, scanned, s - 1)
                nc.vector.tensor_tensor(drive[:, n % 2, :, :], du[:, d, :, :],
                                        b_all[:, n % 2:n % 2 + 1, :].to_broadcast([P, H2, L]), ALU.mult
                                        ).then_inc(drive_done, 1)

            def dve_scan(U, d, n):
                s = STATES * U + n
                nc.vector.wait_ge(decay_done, s + 1)
                nc.vector.wait_ge(drive_done, s + 1)
                wait(nc.vector, g_used, s - 7)
                way = slice(None) if d == 0 else slice(None, None, -1)
                for k in range(H2):
                    last = nc.vector.tensor_tensor_scan(g[:, n % 8, k, way], decay[:, n % 4, k, way],
                                                        drive[:, n % 2, k, way], 0.0, ALU.mult, ALU.add)
                last.then_inc(scanned, 1)

            def dve_gated(U, d):
                nc.vector.wait_ge(y_done, U + 1)
                wait(nc.vector, o_summed, U)
                nc.vector.tensor_tensor(gated[:, :, :], y[:, :, :], sz[:, d, :, :], ALU.mult).then_inc(gated_done, 1)

            def dve_o(b, d, U):
                nc.vector.wait_ge(o_summed, U + 1)
                wait(nc.vector, p_summed, b)
                nc.vector.tensor_tensor(o[:, d, :], bank[:, 0, :], h_of(b), ALU.add).then_inc(o_done, 1)

            def dve_unit(b, d, first, last_unit):
                U = 2 * b + d
                nd = 1 - d
                nc.vector.wait_ge(du_done, U + 1)
                dve_drive(U, d, 0)
                for n in range(STATES):
                    if n + 1 < STATES:
                        dve_drive(U, d, n + 1)
                    dve_scan(U, d, n)
                    if n == 2 and not first:
                        dve_gated(U - 1, nd)
                    if n == 4 and not first:
                        dve_o(b if d == 1 else b - 1, nd, U - 1)
                    if last_unit:
                        continue
                    if n == 9:
                        dve_parts(nd, U + 1)
                    if 10 <= n < 10 + len(LOG1P):
                        dve_factor(nd, U + 1, n - 10)
                    if n == 10 + len(LOG1P):
                        dve_delta(nd, U + 1)

            def pool_unit(b, d):
                U = 2 * b + d
                for n in range(STATES):
                    s = STATES * U + n
                    nc.gpsimd.wait_ge(scanned, s + 1)
                    nc.gpsimd.wait_ge(c_copied, s + 1)
                    nc.gpsimd.tensor_tensor(g[:, n % 8, :, :], g[:, n % 8, :, :],
                                            c_copy[:, n % 4:n % 4 + 1, :].to_broadcast([P, H2, L]), ALU.mult
                                            ).then_inc(g_done, 1)
                    if n - 1 in PAIRED:
                        nc.gpsimd.wait_ge(g_done, s + 1)
                        nc.gpsimd.tensor_tensor(g[:, n % 8, :, :], g[:, n % 8, :, :], g[:, (n - 1) % 8, :, :], ALU.add
                                                ).then_inc(paired, 1)

            block = inner.enter_context(nc.Block())

            @block.tensor
            def _(pe):
                pe_conv(0, 0, 1)
                pe_conv(0, 0, 0)
                pe_z(0, 0, 0)
                pe_xproj(0, 0)
                pe_dpre(0, 0)
                pe_spread(0, 0, 0)
                pe_unit(0, 0, True, False)
                pe_unit(0, 1, False, False)
                with pe.Fori(0, NB - 2) as i:
                    pe_unit(i + 1, 0, False, False)
                    pe_unit(i + 1, 1, False, False)
                pe_unit(NB - 1, 0, False, False)
                pe_unit(NB - 1, 1, False, True)
                for n in range(STATES - LAG, STATES):
                    pe_gate_sum(UNITS - 1, 1, n)
                pe_out(UNITS - 1, 1)
                pe_project(NB - 1, UNITS - 1)

            @block.scalar
            def _(act):
                act_silu(0, 0)
                act_copy_xproj(0)
                act_soft(0, 0)
                for q in range(len(LOG1P)):
                    act_square(0, q)
                act_unit(0, 0, True, False)
                act_unit(0, 1, False, False)
                with act.Fori(0, NB - 2) as i:
                    act_unit(i + 1, 0, False, False)
                    act_unit(i + 1, 1, False, False)
                act_unit(NB - 1, 0, False, False)
                act_unit(NB - 1, 1, False, True)
                act.wait_ge(p_summed, NB)
                nc.scalar.activation(out_of(NB - 1), bank[:, 0, :], ACT.Identity, bias=small[:, 0:1]).then_inc(p_done, 1)

            @block.vector
            def _(dve):
                dve_parts(0, 0)
                for q in range(len(LOG1P)):
                    dve_factor(0, 0, q)
                dve_delta(0, 0)
                dve_unit(0, 0, True, False)
                dve_unit(0, 1, False, False)
                with dve.Fori(0, NB - 2) as i:
                    dve_unit(i + 1, 0, False, False)
                    dve_unit(i + 1, 1, False, False)
                dve_unit(NB - 1, 0, False, False)
                dve_unit(NB - 1, 1, False, True)
                dve_gated(UNITS - 1, 1)
                dve_o(NB - 1, 1, UNITS - 1)

            @block.gpsimd
            def _(pool):
                pool_unit(0, 0)
                pool_unit(0, 1)
                with pool.Fori(0, NB - 1) as i:
                    pool_unit(i + 1, 0)
                    pool_unit(i + 1, 1)

        def finish(dve, c):
            nc.vector.scalar_tensor_tensor(S.x[:, chunk(c)], S.h[:, chunk(c)], small[:, 1:2], S.x[:, chunk(c)],
                                           ALU.mult, ALU.add).then_inc(stepped, 1)
            dve.wait_ge(stepped, c + 1)
            nc.vector.tensor_scalar(S.x[:, chunk(c)], S.x[:, chunk(c)], small[:, 2:3], None, ALU.add)

        layer_norm(nc, S, out, S.h, finish)


def layer3_attention(nc, S, inp):
    sem = S.sem
    scale = float(D) ** -0.5
    with ExitStack() as ctx:
        def sb(n, shape, dt=F32):
            return ctx.enter_context(nc.sbuf_tensor(f"a3_{n}", shape, dt))

        wq, wk, wv = sb("wq", [D, D]), sb("wk", [D, D]), sb("wv", [D, D])
        q, km, v = sb("q", [P, NB, L]), sb("km", [P, NB, L]), sb("v", [P, NB, L])
        attn = sb("attn", [P, NB, TC, L])
        loaded, h_copied, projected, copied = sem("a3_loaded"), sem("a3_h"), sem("a3_projected"), sem("a3_copied")
        cleared = sem("a3_cleared")
        with ExitStack() as inner:
            hc = [inner.enter_context(nc.sbuf_tensor(f"a3_hc{k}", [P, L], F32)) for k in range(2)]
            bank = inner.enter_context(nc.psum_tensor("a3_bank", [P, 6, L], F32))
            block = inner.enter_context(nc.Block())

            @block.sync
            def _(sp):
                for w, name in ((wq, inp["a3_WqT"]), (wk, inp["a3_WkT"]), (wv, inp["a3_WvT"])):
                    sp.dma_start(w[:, :], name).then_inc(loaded, 16)

            @block.gpsimd
            def _(pool):
                with pool.Fori(0, NB // 2) as i:
                    for k in range(2):
                        c = 2 * i + k
                        pool.wait_ge(projected, 3 * c + 3)
                        alone(pool, S)
                        nc.gpsimd.tensor_copy(hc[k][:, :], S.h[:, chunk(c)]).then_inc(h_copied, 1)
                nc.gpsimd.memset(attn[:, :, :, :], 1e-9).then_inc(cleared, 1)

            @block.tensor
            def _(pe):
                pe.sem_inc(projected, 6)
                pe.wait_ge(loaded, 48)
                with pe.Fori(0, NB // 2) as i:
                    for k in range(2):
                        c = 2 * i + k
                        pe.wait_ge(copied, 3 * c + 1)
                        nc.tensor.matmul(bank[:, 3 * k, :], wq[:, :], S.h[:, chunk(c)], start=True, stop=True
                                         ).then_inc(projected, 1)
                        pe.wait_ge(h_copied, c + 1)
                        pe.wait_ge(copied, 3 * c + 2)
                        for j in range(TC):
                            last = nc.tensor.matmul(bank[:, 3 * k + 1, j * P:(j + 1) * P], hc[k][:, j::TC], wk[:, :],
                                                    start=True, stop=True)
                        last.then_inc(projected, 1)
                        pe.wait_ge(copied, 3 * c + 3)
                        for t in range(TC):
                            last = nc.tensor.matmul(bank[:, 3 * k + 2, t * P:(t + 1) * P],
                                                    hc[k][:, t * P:(t + 1) * P], wv[:, :], start=True, stop=True)
                        last.then_inc(projected, 1)

            @block.scalar
            def _(act):
                act.sem_inc(copied, 6)
                with act.Fori(0, NB // 2) as i:
                    for k in range(2):
                        c = 2 * i + k
                        for n, dst in enumerate((q, km, v)):
                            act.wait_ge(projected, 3 * c + 6 + n + 1)
                            nc.scalar.activation(dst[:, bass.ds(c, 1), :].rearrange("p o n -> p (o n)"),
                                                 bank[:, 3 * k + n, :], ACT.Copy).then_inc(copied, 1)

        W = 2 * P
        units = [(j, s0, min(W, L - s0)) for j in range(TC) for s0 in range(j * P, L, W)]
        scored, centred, expd, step, divided, masked = (sem(f"a3_{n}") for n in
                                                        ("scored", "centred", "expd", "step", "divided", "masked"))
        with ExitStack() as inner:
            sc = inner.enter_context(nc.psum_tensor("a3_sc", [P, 2, NB, W], F32))
            top = inner.enter_context(nc.sbuf_tensor("a3_top", [P, W], F32))
            total = inner.enter_context(nc.sbuf_tensor("a3_total", [P, W], F32))
            e = inner.enter_context(nc.sbuf_tensor("a3_e", [P, 2, NB, W], F32))
            block = inner.enter_context(nc.Block())

            def over_batches(col, w):
                return col[:, 0:w].rearrange("p (o w) -> p o w", o=1).to_broadcast([P, NB, w])

            @block.tensor
            def _(pe):
                for n, (j, s0, w) in enumerate(units):
                    if n >= 2:
                        pe.wait_ge(centred, n - 1)
                    for b in range(NB):
                        last = nc.tensor.matmul(sc[:, n % 2, b, 0:w], km[:, b, j * P:(j + 1) * P], q[:, b, s0:s0 + w],
                                                start=True, stop=True)
                    last.then_inc(scored, 1)

            @block.scalar
            def _(act):
                for n, (j, s0, w) in enumerate(units):
                    act.wait_ge(centred, n + 1)
                    nc.scalar.activation(e[:, n % 2, :, 0:w], e[:, n % 2, :, 0:w], ACT.Exp, scale=scale).then_inc(expd, 1)

            @block.vector
            def _(dve):
                chain = Chain(dve, step)

                def centre(n):
                    j, s0, w = units[n]
                    dve.wait_ge(scored, n + 1)
                    if n >= 1:
                        dve.wait_ge(centred, n)
                    chain(nc.vector.tensor_reduce(top[:, 0:w], sc[:, n % 2, :, 0:w].rearrange("p b w -> p w b"),
                                                  AX.X, ALU.max))
                    nc.vector.tensor_tensor(e[:, n % 2, :, 0:w], sc[:, n % 2, :, 0:w], over_batches(top, w),
                                            ALU.subtract).then_inc(centred, 1)

                def divide(n):
                    j, s0, w = units[n]
                    dve.wait_ge(expd, n + 1)
                    if n >= 1:
                        dve.wait_ge(divided, n)
                    chain(nc.vector.tensor_reduce(total[:, 0:w], e[:, n % 2, :, 0:w].rearrange("p b w -> p w b"),
                                                  AX.X, ALU.add))
                    chain(nc.vector.reciprocal(total[:, 0:w], total[:, 0:w]))
                    nc.vector.tensor_tensor(attn[:, :, j, s0:s0 + w], e[:, n % 2, :, 0:w], over_batches(total, w),
                                            ALU.mult).then_inc(divided, 1)

                centre(0)
                for n in range(len(units)):
                    if n + 1 < len(units):
                        centre(n + 1)
                    divide(n)

            @block.gpsimd
            def _(pool):
                for j in range(TC):
                    pool.wait_ge(divided, [u[0] for u in units].index(j) + 1)
                    diagonal = attn[:, :, j, j * P:(j + 1) * P]
                    nc.gpsimd.affine_select(out=diagonal, in_=diagonal, compare_op=ALU.is_ge, fill=1e-9, base=0,
                                            pattern=[[0, NB], [1, P]], channel_multiplier=-1).then_inc(masked, 1)

        summed, added = sem("a3_summed"), sem("a3_added")
        with ExitStack() as inner:
            y = inner.enter_context(nc.psum_tensor("a3_y", [P, 4, L], F32))
            block = inner.enter_context(nc.Block())

            @block.tensor
            def _(pe):
                pe.wait_ge(masked, TC)
                for b in range(NB):
                    if b >= 4:
                        pe.wait_ge(added, b - 3)
                    for j in range(TC):
                        last = nc.tensor.matmul(y[:, b % 4, :], v[:, b, j * P:(j + 1) * P], attn[:, b, j, :],
                                                start=(j == 0), stop=(j == TC - 1))
                    last.then_inc(summed, 1)

            @block.vector
            def _(dve):
                for b in range(NB):
                    dve.wait_ge(summed, b + 1)
                    nc.vector.tensor_tensor(S.x[:, b * L:(b + 1) * L], S.x[:, b * L:(b + 1) * L], y[:, b % 4, :],
                                            ALU.add).then_inc(added, 1)


class Mixture:
    pass


class Unit:

    def __init__(self, w1, w2, gate, gate_key, up=None, bias=None, scale=None):
        self.w1, self.w2, self.gate, self.gate_key = w1, w2, gate, gate_key
        self.up, self.bias, self.scale = up, bias, scale


def new_mixture(S, name, kind, E, EG, K, func, units, factor=1.0, prep_steps=0):
    sem = S.sem
    f = Mixture()
    f.name, f.kind, f.E, f.EG, f.K, f.func, f.factor, f.prep_steps = name, kind, E, EG, K, func, factor, prep_steps
    f.loaded = sem(f"{name}_loaded")
    f.logits_done = sem(f"{name}_logits_done")
    f.score_done = sem(f"{name}_score_done")
    f.shifted_done = sem(f"{name}_shifted_done")
    f.parts_cleared = sem(f"{name}_parts_cleared")
    f.parts_done = sem(f"{name}_parts_done")
    f.turned_done = sem(f"{name}_turned_done")
    f.turned_copied = sem(f"{name}_turned_copied")
    f.turned_copied_f = sem(f"{name}_turned_copied_f")
    f.step = sem(f"{name}_step")
    f.hidden = sem(f"{name}_hidden")
    f.activated = sem(f"{name}_activated")
    f.multiplied = sem(f"{name}_multiplied") if func == ACT.Silu and kind == "sigmoid_bias" else None
    f.scaled = sem(f"{name}_scaled")
    f.used = sem(f"{name}_used")
    f.spread_done = sem(f"{name}_spread_done")
    f.summed = sem(f"{name}_summed")
    f.added = sem(f"{name}_added")
    f.b2 = None
    f.primes = [(s, units) for s in (f.activated, f.multiplied, f.scaled, f.used) if s is not None] + [(f.added, 1)]
    f.n_loads = 0
    return f


def across(src, n, lo=0):
    return src[lo:lo + n].rearrange("(o n) -> o n", o=1).to_broadcast([P, n])


def load(S, f, dst, src):
    f.n_loads += 1
    S.pending.append((dst, src, f.loaded))


def load_b2(S, f, b2, src, E, shared=None):
    for part in range(3):
        load(S, f, b2[SELW * part:SELW * part + E, :], src)
        if shared is not None:
            load(S, f, b2[SELW * part + E:SELW * part + E + 1, :], shared.rearrange("(o n) -> o n", o=1))
    S.clears.append(b2)
    f.b2 = b2[:, :]


def mixture_0(S, inp, sb):
    E, HT = 8, 4
    f = new_mixture(S, "f0", "mask", E, E, 2, ACT.Silu, E * HT, prep_steps=10)
    f.w1, f.w2 = sb("f0_w1", [P, E * HT * P]), sb("f0_w2", [P, E * HT * D])
    router, b1 = sb("f0_router", [D, E]), sb("f0_b1", [P, E * HT])
    g1, g2, rg, rb = sb("f0_g1", [P, E * HT]), sb("f0_g2", [P, E * D]), sb("f0_rg", [P, E]), sb("f0_rb", [P, E])
    b2 = sb("f0_b2", [96, D])
    f.scale1 = sb("f0_scale1", [P, E * HT])
    load_b2(S, f, b2, inp["L0_ffn_b2"], E)
    load(S, f, f.w1[:, :], inp["f0_w1T"])
    load(S, f, f.w2[:, :], inp["f0_w2T"])
    load(S, f, router[:, :], inp["f0_routerT"])
    load(S, f, b1[:, :], inp["f0_b1T"])
    load(S, f, g1[:, :], inp["f0_g1T"])
    load(S, f, g2[:, :], across(inp["f0_g2"], E * D))
    load(S, f, rg[:, :], across(inp["L0_ffn_gate_g"], E))
    load(S, f, rb[:, :], across(inp["L0_ffn_gate_b"], E))
    f.router, f.router_bias, f.router_gain, f.g1, f.g2 = router[:, :], rb[:, :], rg[:, :], g1[:, :], g2[:, :]
    f.prep_done, f.wn_squared = S.sem("f0_prep_done"), S.sem("f0_wn_squared")
    f.wn_summed, f.wn_rooted = S.sem("f0_wn_summed"), S.sem("f0_wn_rooted")
    f.units = [Unit(f.w1[:, u * P:(u + 1) * P], f.w2[:, u * D:(u + 1) * D], S.sel[:, u // HT, :], u // HT,
                    bias=b1[:, u:u + 1], scale=f.scale1[:, u:u + 1]) for u in range(E * HT)]
    return f


def mixture_1(S, inp, sb):
    E, HT = 6, 2
    f = new_mixture(S, "f1", "softmax", E, E, 2, ACT.Gelu, E * HT)
    w1, w2 = sb("f1_w1", [P, E * HT * P]), sb("f1_w2", [P, E * HT * D])
    router, b1, rb, b2 = sb("f1_router", [D, E]), sb("f1_b1", [P, E * HT]), sb("f1_rb", [P, E]), sb("f1_b2", [96, D])
    load_b2(S, f, b2, inp["L1_ffn_b2"], E)
    load(S, f, w1[:, :], inp["f1_w1T"])
    load(S, f, w2[:, :], inp["f1_w2T"])
    load(S, f, router[:, :], inp["L1_ffn_Wg"])
    load(S, f, b1[:, :], inp["f1_b1T"])
    load(S, f, rb[:, :], across(inp["L1_ffn_bg"], E))
    f.router, f.router_bias = router[:, :], rb[:, :]
    f.units = [Unit(w1[:, u * P:(u + 1) * P], w2[:, u * D:(u + 1) * D], S.sel[:, u // HT, :], u // HT,
                    bias=b1[:, u:u + 1]) for u in range(E * HT)]
    return f


def mixture_2(S, inp, sb):
    E, H = 8, 64
    f = new_mixture(S, "f2", "sigmoid", E, E + 1, 2, ACT.Gelu, E // 2 + 1)
    w1, w2 = sb("f2_w1", [P, (E + 2) * H]), sb("f2_w2", [P, (E // 2 + 1) * D])
    router, b1, b2 = sb("f2_router", [D, E]), sb("f2_b1", [P, E // 2 + 1]), sb("f2_b2", [96, D])
    scale = sb("f2_scale", [P, 1])
    load_b2(S, f, b2, inp["L2_ffn_b2"], E, inp["L2_ffn_bs2"])
    load(S, f, w1[:, 0:E * H], inp["f2_w1T"])
    load(S, f, w1[:, E * H:(E + 1) * H], inp["L2_ffn_Ws1"])
    load(S, f, w2[:, 0:E // 2 * D], inp["f2_w2T"])
    load(S, f, w2[0:H, E // 2 * D:], inp["L2_ffn_Ws2"])
    S.clears += [w1, w2, b1]
    load(S, f, router[:, :], inp["L2_ffn_gate_W"])
    load(S, f, b1[:, 0:E // 2], inp["f2_b1T"])
    load(S, f, b1[0:H, E // 2:], inp["L2_ffn_bs1"].rearrange("(p o) -> p o", o=1))
    load(S, f, scale[:, :], across(inp["f2_route_scale"], 1))
    f.router, f.route_scale = router[:, :], scale[:, 0:1]
    spread = [S.sel_pair[:, u, :] for u in range(E // 2)] + [S.sel[:, E, :]]
    f.units = [Unit(w1[:, u * P:(u + 1) * P], w2[:, u * D:(u + 1) * D], spread[u], u, bias=b1[:, u:u + 1])
               for u in range(E // 2 + 1)]
    return f


def mixture_3(S, inp, sb):
    E = 16
    f = new_mixture(S, "f3", "sigmoid_bias", E, E + 1, 8, ACT.Silu, E + 1, factor=2.826)
    wg, wu, wd = (sb(f"f3_{n}", [P, (E + 1) * P]) for n in ("wg", "wu", "wd"))
    router, rb = sb("f3_router", [D, E]), sb("f3_rb", [P, E])
    for w, routed, shared in ((wg, "f3_wgT", "f3_sgT"), (wu, "f3_wuT", "f3_suT"), (wd, "f3_wdT", "f3_sdT")):
        load(S, f, w[:, 0:E * P], inp[routed])
        load(S, f, w[:, E * P:], inp[shared])
    load(S, f, router[:, :], inp["f3_routerT"])
    load(S, f, rb[:, :], across(inp["L3_ffn_expert_bias"], E))
    f.router, f.router_bias = router[:, :], rb[:, :]
    f.units = [Unit(wg[:, u * P:(u + 1) * P], wd[:, u * P:(u + 1) * P], S.sel[:, u, :], u,
                    up=wu[:, u * P:(u + 1) * P]) for u in range(E + 1)]
    return f


def mixture(nc, S, f, h):
    with ExitStack() as ctx:
        f.gates_b = ctx.enter_context(nc.sbuf_tensor(f"{f.name}_gates_b", [96, T], BF16))
        f.gates_f = ctx.enter_context(nc.sbuf_tensor(f"{f.name}_gates_f", [96, T], F32))
        if f.kind == "mask":
            normalise_weights(nc, S, f)
        gates(nc, S, f, h)
        experts(nc, S, f, h)


def build(nc, inp, out, stages):
    S = State()
    with ExitStack() as ctx:
        def sb(name, shape, dt=F32):
            return ctx.enter_context(nc.sbuf_tensor(name, shape, dt))

        def sem(name):
            handle = nc.alloc_semaphore(name=name)
            handles.append(handle)
            return handle

        handles = []
        S.sem = sem
        S.pending, S.clears, S.primes, S.setup_primes = [], [], [], []
        S.ln_calls = 0
        S.x = sb("x", [D, T])
        S.h = sb("h", [D, T])
        S.ones, S.mean_w, S.eps = sb("ones", [P, P]), sb("mean_w", [P, P]), sb("eps", [P, 1])
        S.ident, S.ident_b = sb("ident", [P, P]), sb("ident_b", [P, P], BF16)
        S.sel, S.sel_pair = sb("sel", [96, SELW, P], BF16), sb("sel_pair", [96, 4, P], BF16)
        S.x_loaded, S.setup_step, S.cleared = sem("x_loaded"), sem("setup_step"), sem("cleared")
        S.stored, S.passed = sem("stored"), sem("passed")
        S.ln_mean, S.ln_centered, S.ln_squared, S.ln_var = (sem(f"ln_{n}") for n in ("mean", "centered", "squared", "var"))
        S.ln_std, S.ln_rstd, S.ln_rows, S.ln_spread = (sem(f"ln_{n}") for n in ("std", "rstd", "rows", "spread"))
        S.ln_normed, S.ln_step, S.ln_turned = sem("ln_normed"), sem("ln_step"), sem("ln_turned")

        n_lasting = len(handles)
        first = ExitStack()

        def sb_first(name, shape, dt=F32):
            return first.enter_context(nc.sbuf_tensor(name, shape, dt))

        if "a0" in stages or "a1" in stages:
            attention_semaphores(S)
            projection_semaphores(S)
            pattention_semaphores(S)
        S.w_mem, S.w_dot = sb("w_mem", [P, 1]), sb("w_dot", [P, 1])
        fs = {}
        if "f0" in stages:
            fs["f0"] = mixture_0(S, inp, sb_first)
        stage_setup(nc, S, inp, fs)
        if "a0" in stages:
            layer_norm(nc, S, S.x, S.h)
            layer0_attention(nc, S, inp)
        if "f0" in stages:
            layer_norm(nc, S, S.x, S.h)
            mixture(nc, S, fs["f0"], S.h)
        first.close()
        middle = ExitStack()

        def sb_middle(name, shape, dt=F32):
            return middle.enter_context(nc.sbuf_tensor(name, shape, dt))

        if "f1" in stages:
            fs["f1"] = mixture_1(S, inp, sb_middle)
            S.primes += fs["f1"].primes
        if "a1" in stages:
            layer_norm(nc, S, S.x, S.h)
            layer1_attention(nc, S, inp)
        if "f1" in stages:
            layer_norm(nc, S, S.x, S.h)
            mixture(nc, S, fs["f1"], S.h)
        middle.close()
        nc.clear_and_free_semaphores([s for s in handles[n_lasting:]])
        nc.all_engine_barrier()
        if "a2" in stages:
            layer_norm(nc, S, S.x, S.h)
            layer2_mamba(nc, S, inp)
        last = ExitStack()

        def sb_last(name, shape, dt=F32):
            return last.enter_context(nc.sbuf_tensor(name, shape, dt))

        if "f2" in stages:
            fs["f2"] = mixture_2(S, inp, sb_last)
        if "f3" in stages:
            fs["f3"] = mixture_3(S, inp, sb_last)
        for n in ("f2", "f3"):
            if n in fs:
                S.primes += fs[n].primes
        if "f2" in stages:
            layer_norm(nc, S, S.x, S.h)
            mixture(nc, S, fs["f2"], S.h)
        if "a3" in stages:
            layer_norm(nc, S, S.x, S.h)
            layer3_attention(nc, S, inp)
        if "f3" in stages:
            layer_norm(nc, S, S.x, S.h)
            mixture(nc, S, fs["f3"], S.h)
        with nc.Block() as block:
            @block.sync
            def _(sp):
                sp.dma_start(out, S.x[:, :]).then_inc(S.stored, 16)
                sp.wait_ge(S.stored, 16)
        last.close()


USED = ['L0_attn_Wk', 'L0_attn_Wq', 'L0_attn_Wv', 'L0_attn_memory', 'L0_attn_memory_norm', 'L0_attn_memory_weight', 'L0_ffn_b2', 'L0_ffn_gate_b', 'L0_ffn_gate_g', 'L1_attn_fV', 'L1_attn_kV', 'L1_attn_pV', 'L1_attn_qV', 'L1_attn_vV', 'L1_ffn_Wg', 'L1_ffn_b2', 'L1_ffn_bg', 'L2_ffn_Ws1', 'L2_ffn_Ws2', 'L2_ffn_b2', 'L2_ffn_bs1', 'L2_ffn_bs2', 'L2_ffn_gate_W', 'L3_ffn_expert_bias', 'a1_fKT', 'a1_kKT', 'a1_pKT', 'a1_qKT', 'a1_vKT', 'a2_bw_convT', 'a2_bw_dtT', 'a2_bw_packT', 'a2_fw_convT', 'a2_fw_dtT', 'a2_fw_packT', 'a2_projT', 'a2_smallT', 'a3_WkT', 'a3_WqT', 'a3_WvT', 'f0_b1T', 'f0_g1T', 'f0_g2', 'f0_routerT', 'f0_w1T', 'f0_w2T', 'f1_b1T', 'f1_w1T', 'f1_w2T', 'f2_b1T', 'f2_route_scale', 'f2_w1T', 'f2_w2T', 'f3_routerT', 'f3_sdT', 'f3_sgT', 'f3_suT', 'f3_wdT', 'f3_wgT', 'f3_wuT', 'xT']


def lay_out(i):
    import numpy as np

    def tiles(a, E, HT):
        return a.reshape(E, HT, P).transpose(2, 0, 1).reshape(P, E * HT)

    def rows(a):
        return a.transpose(2, 0, 1).reshape(a.shape[2], -1)

    d = dict(i)
    d["xT"] = i["L0_attn_x"].reshape(T, D).T
    d["f0_w1T"] = rows(i["L0_ffn_w1_v"])
    d["f0_w2T"] = i["L0_ffn_w2_v"].reshape(8, D, 4, P).transpose(3, 0, 2, 1).reshape(P, -1)
    d["f0_routerT"] = i["L0_ffn_gate_v"].T
    d["f0_b1T"] = tiles(i["L0_ffn_b1"], 8, 4)
    d["f0_g1T"] = tiles(i["L0_ffn_w1_g"], 8, 4)
    d["f0_g2"] = i["L0_ffn_w2_g"].reshape(-1)
    d["a1_qKT"], d["a1_kKT"], d["a1_vKT"], d["a1_pKT"], d["a1_fKT"] = (i[f"L1_attn_{n}K"].T for n in "qkvpf")
    d["a3_WqT"], d["a3_WkT"], d["a3_WvT"] = (i[f"L3_attn_W{n}"].T for n in "qkv")
    d["f1_w1T"] = i["L1_ffn_W1"].transpose(1, 0, 2).reshape(D, -1)
    d["f1_w2T"] = i["L1_ffn_W2"].reshape(6, 2, P, D).transpose(2, 0, 1, 3).reshape(P, -1)
    d["f1_b1T"] = tiles(i["L1_ffn_b1"], 6, 2)
    d["f2_w1T"] = i["L2_ffn_W1"].transpose(1, 0, 2).reshape(D, -1)
    d["f2_w2T"] = i["L2_ffn_W2"].reshape(4, P, D).transpose(1, 0, 2).reshape(P, -1)
    d["f2_b1T"] = i["L2_ffn_b1"].reshape(4, P).T
    d["f2_route_scale"] = i["L2_ffn_route_scale"].reshape(1)
    d["f3_routerT"] = i["L3_ffn_gate_w"].T
    d["f3_wgT"], d["f3_wuT"], d["f3_wdT"] = (rows(i[f"L3_ffn_w_{n}"]) for n in ("gate", "up", "down"))
    d["f3_sgT"], d["f3_suT"], d["f3_sdT"] = (i[f"L3_ffn_shared_{n}_w"].T for n in ("gate", "up", "down"))

    def halves(a):
        return a.reshape(2, P, -1).transpose(1, 0, 2).reshape(P, -1)

    def packed(w):
        xproj = w("xproj_w").T
        bc = np.concatenate([xproj[:, 8:]] * 3 + [xproj[:, :8]], axis=1)
        return np.concatenate([w("in_w").T, halves(bc), halves(w("out_w").T), halves(w("dt_b")),
                               halves(w("conv_b")), halves(w("Dp")), halves(w("Alog"))], axis=1)

    d["a2_fw_packT"] = packed(lambda n: i["L2_attn_fw_" + n])
    d["a2_bw_packT"] = packed(lambda n: i["L2_attn_bw_" + n])
    d["a2_fw_convT"], d["a2_bw_convT"] = (i[f"L2_attn_{n}_conv_w"].reshape(2 * D, 4).T.reshape(-1) for n in ("fw", "bw"))
    d["a2_fw_dtT"], d["a2_bw_dtT"] = (i[f"L2_attn_{n}_dt_w"].T for n in ("fw", "bw"))
    d["a2_projT"] = halves(i["L2_attn_proj_w"].T)
    d["a2_smallT"] = np.stack([i[f"L2_attn_{n}"] for n in ("proj_b", "ln_w", "ln_b")], axis=1)
    return {k: np.ascontiguousarray(v) for k, v in d.items() if k in USED}


def kernel(**inputs):
    import numpy as _np
    import concourse.bacc as _bacc
    from concourse import mybir as _mybir
    from concourse.bass_utils import run_bass_kernel_spmd as _run

    nc = _bacc.Bacc("TRN2", target_bir_lowering=False, num_devices=1)
    laid = lay_out({k: _np.asarray(v) for k, v in inputs.items()})
    arrays, aps = {}, {}
    for name, a in laid.items():
        arrays[f"in_{name}"] = a
        aps[name] = nc.dram_tensor(f"in_{name}", a.shape, _mybir.dt.from_np(a.dtype), kind="ExternalInput").ap()
    out = nc.dram_tensor("out_xT", (D, T), F32, kind="ExternalOutput").ap()
    build(nc, aps, out, STAGES)
    r = _run(nc, [arrays], core_ids=[0])
    return _np.ascontiguousarray(r.results[0]["out_xT"].T).reshape(NB, L, D)
```
